# Optimizing a Trainium2 kernel written in Bass

```python
import numpy as np
import jax
import jax.numpy as jnp

def _softmax(x, axis=-1):
    return jax.nn.softmax(x, axis=axis)

def _gelu(x):
    return jax.nn.gelu(x, approximate=True)

def _silu(x):
    return jax.nn.silu(x)

def _sigmoid(x):
    return jax.nn.sigmoid(x)

def _layernorm(x, axis=-1, eps=1e-05):
    m = jnp.mean(x, axis=axis, keepdims=True)
    v = jnp.var(x, axis=axis, keepdims=True)
    return (x - m) / jnp.sqrt(v + eps)

def _scatter_add(tgt, idx, src, axis=0):
    return tgt.at[idx].add(src)

def _segment_sum(src, seg, n):
    return jax.ops.segment_sum(src, seg, n)
kernel_name = 'mk_seq_postln_d1_jaxref_r8_5803a8'

def setup_inputs(seed: int=0):
    np.random.seed(seed)
    _w = jnp.asarray

    def _L0_attn_setup():
        import jax, jax.numpy as jnp
        import numpy as np
        DIM = 128
        HEADS = 16
        HEAD_DIM = DIM // HEADS

        def feature_map(x):
            return jnp.where(x > 0, x + 1.0, jnp.exp(x))
        key = jax.random.key(seed)
        ks = jax.random.split(key, 11)
        B, N, D = (4, 1024, DIM)
        s = 1.0 / np.sqrt(D)
        inp = {'x': jax.random.normal(ks[0], (B, N, D), dtype=jnp.float32), 'wg_w': jax.random.normal(ks[1], (D, D), dtype=jnp.float32) * s, 'wg_b': jnp.zeros((D,), dtype=jnp.float32), 'wq_w': jax.random.normal(ks[2], (D, D), dtype=jnp.float32) * s, 'wq_b': jnp.zeros((D,), dtype=jnp.float32), 'wk_w': jax.random.normal(ks[3], (D, D), dtype=jnp.float32) * s, 'wk_b': jnp.zeros((D,), dtype=jnp.float32), 'wv_w': jax.random.normal(ks[4], (D, D), dtype=jnp.float32) * s, 'wv_b': jnp.zeros((D,), dtype=jnp.float32), 'out_w': jax.random.normal(ks[5], (D, D), dtype=jnp.float32) * s, 'out_b': jnp.zeros((D,), dtype=jnp.float32)}
        return inp
    _L0_attn_in = _L0_attn_setup()

    def _L0_ffn_setup():
        import jax, jax.numpy as jnp
        import numpy as np
        E = 16
        F_C = 2.0
        D = 128
        I = 4 * D
        IS = 2 * D
        B, S = (4, 128)
        key = jax.random.key(seed)
        ks = jax.random.split(key, 8)
        w = 0.02
        return {'hidden_states': jax.random.normal(ks[0], (B, S, D), dtype=jnp.float32), 'gate_w': jax.random.normal(ks[1], (E, D), dtype=jnp.float32) * w, 'Wg': jax.random.normal(ks[2], (E, I, D), dtype=jnp.float32) * w, 'Wu': jax.random.normal(ks[3], (E, I, D), dtype=jnp.float32) * w, 'Wd': jax.random.normal(ks[4], (E, D, I), dtype=jnp.float32) * w, 'Sg': jax.random.normal(ks[5], (IS, D), dtype=jnp.float32) * w, 'Su': jax.random.normal(ks[6], (IS, D), dtype=jnp.float32) * w, 'Sd': jax.random.normal(ks[7], (D, IS), dtype=jnp.float32) * w}
    _L0_ffn_in = _L0_ffn_setup()
    _d = {'L0_attn_x': _L0_attn_in['x'], 'L0_attn_wg_w': _L0_attn_in['wg_w'], 'L0_attn_wg_b': _L0_attn_in['wg_b'], 'L0_attn_wq_w': _L0_attn_in['wq_w'], 'L0_attn_wq_b': _L0_attn_in['wq_b'], 'L0_attn_wk_w': _L0_attn_in['wk_w'], 'L0_attn_wk_b': _L0_attn_in['wk_b'], 'L0_attn_wv_w': _L0_attn_in['wv_w'], 'L0_attn_wv_b': _L0_attn_in['wv_b'], 'L0_attn_out_w': _L0_attn_in['out_w'], 'L0_attn_out_b': _L0_attn_in['out_b'], 'L0_ffn_gate_w': _L0_ffn_in['gate_w'], 'L0_ffn_Wg': _L0_ffn_in['Wg'], 'L0_ffn_Wu': _L0_ffn_in['Wu'], 'L0_ffn_Wd': _L0_ffn_in['Wd'], 'L0_ffn_Sg': _L0_ffn_in['Sg'], 'L0_ffn_Su': _L0_ffn_in['Su'], 'L0_ffn_Sd': _L0_ffn_in['Sd']}
    _x0 = _d['L0_attn_x']
    _d['L0_attn_x'] = jax.random.normal(jax.random.fold_in(jax.random.key(seed), 1), (16, 512, 128), dtype=_x0.dtype)
    del _x0
    return _d

def reference(L0_attn_x, L0_attn_wg_w, L0_attn_wg_b, L0_attn_wq_w, L0_attn_wq_b, L0_attn_wk_w, L0_attn_wk_b, L0_attn_wv_w, L0_attn_wv_b, L0_attn_out_w, L0_attn_out_b, L0_ffn_gate_w, L0_ffn_Wg, L0_ffn_Wu, L0_ffn_Wd, L0_ffn_Sg, L0_ffn_Su, L0_ffn_Sd):

    def _L0_attn_ref(x, wg_w, wg_b, wq_w, wq_b, wk_w, wk_b, wv_w, wv_b, out_w, out_b):
        import jax, jax.numpy as jnp
        import numpy as np
        DIM = 128
        HEADS = 16
        HEAD_DIM = DIM // HEADS

        def feature_map(x):
            return jnp.where(x > 0, x + 1.0, jnp.exp(x))
        B, N, D = x.shape
        H, Hd = (HEADS, HEAD_DIM)
        q = (x @ wq_w + wq_b).reshape(B, N, H, Hd)
        k = (x @ wk_w + wk_b).reshape(B, N, H, Hd)
        v = (x @ wv_w + wv_b).reshape(B, N, H, Hd)
        gate = jax.nn.sigmoid(x @ wg_w + wg_b)
        q = feature_map(q)
        k = feature_map(k)
        kv = jnp.einsum('bnhd,bnhe->bhde', k, v)
        z = 1.0 / (jnp.einsum('bnhd,bhd->bnh', q, k.sum(axis=1)) + 1e-06)
        scores = jnp.einsum('bnhd,bhde,bnh->bnhe', q, kv, z)
        out = scores.reshape(B, N, D)
        return gate * out @ out_w + out_b

    def _L0_ffn_ref(hidden_states, gate_w, Wg, Wu, Wd, Sg, Su, Sd):
        import jax, jax.numpy as jnp
        import numpy as np
        E = 16
        F_C = 2.0
        D = 128
        I = 4 * D
        IS = 2 * D
        B, S = (4, 128)
        b, s, d = hidden_states.shape
        T = b * s
        C = int(T * F_C / E)
        flat_x = hidden_states.reshape(T, d)
        logits = flat_x @ gate_w.T
        scores = jax.nn.softmax(logits, axis=-1).T
        topk_weight, topk_idx = jax.lax.top_k(scores, C)
        xg = flat_x[topk_idx]
        g = jnp.einsum('ecd,eid->eci', xg, Wg)
        u = jnp.einsum('ecd,eid->eci', xg, Wu)
        h = jax.nn.gelu(g, approximate=False) * u
        eo = jnp.einsum('eci,edi->ecd', h, Wd)
        eo = eo * topk_weight[..., None]
        flat_out = jnp.zeros_like(flat_x).at[topk_idx.reshape(-1)].add(eo.reshape(-1, d))
        out = flat_out.reshape(b, s, d)
        sg = hidden_states @ Sg.T
        su = hidden_states @ Su.T
        shared = jax.nn.gelu(sg, approximate=False) * su @ Sd.T
        return out + shared
    x = L0_attn_x
    x = _layernorm(x + _L0_attn_ref(x, L0_attn_wg_w, L0_attn_wg_b, L0_attn_wq_w, L0_attn_wq_b, L0_attn_wk_w, L0_attn_wk_b, L0_attn_wv_w, L0_attn_wv_b, L0_attn_out_w, L0_attn_out_b), axis=-1)
    x = _layernorm(x + _L0_ffn_ref(x, L0_ffn_gate_w, L0_ffn_Wg, L0_ffn_Wu, L0_ffn_Wd, L0_ffn_Sg, L0_ffn_Su, L0_ffn_Sd), axis=-1)
    return x

_drawn_inputs = setup_inputs


def setup_inputs(seed=0):
    import zlib

    import numpy as np

    out = dict(_drawn_inputs(seed))
    spreads = {'L0_attn_wg_b': (0.0, 0.8),
     'L0_attn_wq_b': (0.0, 2.0),
     'L0_attn_wk_b': (0.0, 2.0),
     'L0_attn_wv_b': (0.0, 0.1),
     'L0_attn_out_b': (0.0, 0.1)}
    factors = {'L0_attn_wq_w': 7.156,
     'L0_attn_wk_w': 3.725,
     'L0_ffn_gate_w': 8.0,
     'L0_ffn_Wg': 8.0,
     'L0_ffn_Wu': 8.0,
     'L0_ffn_Wd': 8.0,
     'L0_ffn_Sg': 6.856,
     'L0_ffn_Su': 6.731,
     'L0_ffn_Sd': 6.756}
    for name, (base, spread) in spreads.items():
        noise = np.random.default_rng([zlib.crc32(name.encode()), seed]).standard_normal(out[name].shape)
        drawn = base * np.exp(spread * noise) if base else spread * noise
        out[name] = jnp.asarray(drawn.astype(out[name].dtype))
    for name, factor in factors.items():
        out[name] = (out[name] * factor).astype(out[name].dtype)
    return out
```

```python
from contextlib import ExitStack

import numpy as np

import concourse.bass as bass
from concourse import mybir

F32 = mybir.dt.float32
F32R = mybir.dt.float32r
F16 = mybir.dt.float16
I32 = mybir.dt.int32
ACT = mybir.ActivationFunctionType
ALU = mybir.AluOpType
AX = mybir.AxisListType

P = 128
D = 128
HEADS = 16
HD = D // HEADS
NB = 16
SEQ = 512
TPB = SEQ // P
T = NB * SEQ
NT = T // P
E = 16
CAP = 2 * T // E
ST = CAP // P
HALF = CAP // 2
HT = ST // 2
I = 512
IC = I // P
SC = 2
ROW = D + E
NC = NT // 8
LN_EPS = 1e-5
LAG = 2
FT = 8
NG = NT // FT
FG = 4

C_IDENT, C_HEAD, C_SAME, C_PREF, C_UPPER, C_DIFF, C_SEL2, C_SLOT, C_BLK, C_IOTA = np.cumsum(
    [0, P, P, P, P, P, P, HEADS, ST, E]).tolist()
C_END = C_IOTA + CAP


def constants():
    c = np.zeros((P, C_END), np.float32)
    r, q = np.arange(P)[:, None], np.arange(P)[None, :]
    c[:, C_IDENT:C_IDENT + P] = r == q
    c[:, C_HEAD:C_HEAD + P] = r // HD == q // HD
    c[:, C_SAME:C_SAME + P] = r % E == q % E
    c[:, C_PREF:C_PREF + P] = (r % E == q % E) & (r // E < q // E)
    c[:, C_UPPER:C_UPPER + P] = r < q
    c[:, C_DIFF:C_DIFF + P] = (r == q) * 1.0 - (r == q - 1) * 1.0
    c[:, C_SEL2:C_SEL2 + HEADS] = 2.0 * (r // HD == np.arange(HEADS)[None, :])
    c[:, C_SLOT:C_SLOT + ST] = r + P * np.arange(ST)[None, :]
    c[:, C_BLK:C_BLK + E] = r >= 1
    c[:, C_IOTA:C_END] = np.arange(CAP)[None, :]
    return c


def program(nc, x, xT, wq, wkvg, wo, bcols, brow, bo, consts, gateT, wsgu, wsd, wgu, wd, out):
    with ExitStack() as ctx:
        def sb(name, shape, dt=F32):
            return ctx.enter_context(nc.sbuf_tensor(name, shape, dt))

        def region(name, size):
            whole = sb(name, [P, size])

            def layout():
                at = [0]

                def carve(shape, dt=F32):
                    n = int(np.prod(shape[1:]))
                    assert at[0] + n <= size
                    part = whole[:, at[0]:at[0] + n]
                    at[0] += n
                    if dt != F32:
                        part = part.bitcast(dt)
                    dims = "abcd"[:len(shape) - 1]
                    sizes = dict(zip(dims, shape[1:]))
                    return part.rearrange(f"p ({' '.join(dims)}) -> p {' '.join(dims)}", **sizes)

                return carve

            return layout

        def sem(name):
            return ctx.enter_context(nc.semaphore(name))

        def wait(eng, s, v):
            if not (isinstance(v, int) and v <= 0):
                eng.wait_ge(s, v)

        def wait_apart(eng, s, v):
            wait(eng, s, v)
            if not isinstance(v, int):
                eng.sem_inc(s_apart, 1)

        def landed(i, par, ndma=1):
            return 16 * ndma * (i // 2 + 1) if isinstance(i, int) else (i - par) * (8 * ndma) + 16 * ndma

        def live(b, n=NB):
            return not isinstance(b, int) or 0 <= b < n

        def sweep(eng, step, lag):
            for i in range(4):
                step(i, i % 2)
            with eng.Fori(2, NB // 2) as j:
                step(j * 2, 0)
                step(j * 2 + 1, 1)
            for i in range(NB, NB + lag):
                step(i, i % 2)

        rows = nc.dram_tensor("rows", [T, ROW], F32, kind="Internal").ap()
        acc = nc.dram_tensor("acc", [T, D], F32, kind="Internal").ap()
        rows_tok = rows.rearrange("(t p) r -> p t r", p=P)
        acc_tok = acc.rearrange("(t p) d -> p t d", p=P)
        x_tok = x.rearrange("b (t p) d -> p (b t) d", p=P)
        out_tok = out.rearrange("b (t p) d -> p (b t) d", p=P)

        cst = sb("cst", [P, C_END])
        ident = cst[:, C_IDENT:C_IDENT + P]
        headmask = cst[:, C_HEAD:C_HEAD + P]
        same_expert = cst[:, C_SAME:C_SAME + P]
        earlier_run = cst[:, C_PREF:C_PREF + P]
        upper = cst[:, C_UPPER:C_UPPER + P]
        headsel2 = cst[:, C_SEL2:C_SEL2 + HEADS]
        slotno = cst[:, C_SLOT:C_SLOT + ST]
        ident16 = sb("ident16", [P, P], F16)
        diff16 = sb("diff16", [P, P], F16)
        iota16 = sb("iota16", [P, CAP], F16)
        wq_s, wo_s = sb("wq_s", [P, D]), sb("wo_s", [P, D])
        wkvg_s = sb("wkvg_s", [P, 3 * D])
        bcol = sb("bcol", [P, 1])
        q1bias, nqbias = sb("q1bias", [P, 1]), sb("nqbias", [P, 1])
        brow_s = sb("brow_s", [33, 3 * D])
        onesraw = sb("onesraw", [33, P])
        bpair = sb("bpair", [P, 3 * D], F32R)
        onespair = sb("onespair", [P, P], F32R)
        bo_s = sb("bo_s", [P, TPB, D])
        neghalf = sb("neghalf", [P, FT])
        gateT_s = sb("gateT_s", [P, E])
        wsgu_s = sb("wsgu_s", [P, 2, SC * P])
        wsd_s = sb("wsd_s", [P, SC, D])

        work = region("work", 16640)
        at = work()
        xTb = at([P, 2, SEQ])
        xt, xb, x1 = (at([P, 2, TPB, D]) for _ in range(3))
        x1Ts = at([P, 2, SEQ])
        nk, kf, gate = (at([P, 2, TPB, D]) for _ in range(3))
        v1 = at([P, 2, TPB, D + 1])
        nq, qf = at([P, 2, SEQ]), at([P, 2, SEQ])
        kvbd = at([P, 2, D])
        ks16 = at([P, 2, HEADS])
        den, rden = at([P, 2, TPB * HEADS]), at([P, 2, TPB * HEADS])
        y1, y = at([P, 2, TPB, D]), at([P, 2, TPB, D])
        yT = at([P, 2, SEQ])
        bns = at([P, TPB, 6])
        mv = at([P, 2, TPB, 2])
        veps, rstd = at([P, 2, TPB]), at([P, 2, TPB])

        X1 = sb("X1", [P, NT, D])
        feat = region("feat", T)
        X1T = feat()([P, T])
        LG = sb("LG", [P, NT, E])
        S = sb("S", [P, 8, NT // 8, E])
        SE = sb("SE", [P, CAP])
        stat = sb("stat", [P, 3, NT])
        junk = sb("junk", [P, CAP], F16)
        cnt = sb("cnt", [P, 1])
        cand, thr, step_i = sb("cand", [P, 1], I32), sb("thr", [P, 1], I32), sb("step_i", [P, 1], I32)
        bitf, nbit = sb("bitf", [P, 2]), sb("nbit", [P, 2], I32)
        tiecnt = sb("tiecnt", [P, 2])
        need, tieoff = sb("need", [P, 1]), sb("tieoff", [P, 1])
        gtm, eqm, tiesel, sel = (sb(n, [P, CAP], F16) for n in ("gtm", "eqm", "tiesel", "sel"))
        rank = sb("rank", [P, CAP])
        M = sb("M", [P, E, NT])
        G = sb("G", [P, E, NT])
        gprev, nsel, base = (sb(n, [P, E]) for n in ("gprev", "nsel", "base"))
        off = sb("off", [P, E + 1])
        C16 = sb("C16", [P, E, NT], F16)
        tab = sb("tab", [P, E, NT + 1], F16)
        U = sb("U", [P, CAP], F16)

        cmp = sb("cmp", [P, ST, NT])
        cntt = sb("cntt", [P, ST])
        idx = sb("idx", [P, 2, ST], I32)
        idxs = sb("idxs", [P, 2, ST], I32)
        at = work()
        xg = at([P, 2, ST, ROW])
        wgu_s = at([P, 2, 2, I])
        wd_s = at([P, 2, IC, D])
        sgg, suc = at([P, SC, SEQ]), at([P, SC, SEQ])
        hs = at([P, 2, SC, SEQ])
        so = at([P, 2, TPB, D])
        at = feat()
        xgT = at([P, CAP])
        gg = at([P, 2, HALF])
        hT = at([P, IC, CAP])
        eo = at([P, 2, ST, D])

        at = work()
        fbns, fmv = at([P, FT, 6]), at([P, 2, FT, 2])
        fveps, frstd, fshift = (at([P, 2, FT]) for _ in range(3))

        bank = [ctx.enter_context(nc.psum_tensor(f"bank{n}", [P, 512], F32)) for n in range(6)]
        wide = ctx.enter_context(nc.psum_tensor("wide", [P, 2, 512], F32))
        psK, psV, psG, psQ, psN, psOT = bank
        psYT, psKB = wide[:, 0, :], wide[:, 1, :]
        kb_kv, kb_den, kb_lg = psKB[:, 0:D + 1], psKB[:, 192:192 + TPB * HEADS], psKB[:, 256:256 + TPB * E]
        psSG, psSU, psSO, psTOT = bank[0:2], bank[2:4], bank[4], bank[5]
        psX, psGG, psUU = bank[0:2], bank[2:4], bank[4:6]

        s_apart, s_w, s_pool0, s_dve0 = sem("s_apart"), sem("s_w"), sem("s_pool0"), sem("s_dve0")
        s_xT = [sem(f"s_xT{n}") for n in range(2)]
        s_xt = [sem(f"s_xt{n}") for n in range(2)]
        s_kps, s_vps, s_qps, s_gps = (sem(n) for n in ("s_kps", "s_vps", "s_qps", "s_gps"))
        s_nk, s_ek, s_v, s_nq, s_eq, s_gate = (sem(n) for n in ("s_nk", "s_ek", "s_v", "s_nq", "s_eq", "s_gate"))
        s_kf, s_qf, s_xb = sem("s_kf"), sem("s_qf"), sem("s_xb")
        s_kbps, s_kvbd, s_ks16, s_ndps = (sem(n) for n in ("s_kbps", "s_kvbd", "s_ks16", "s_ndps"))
        s_den, s_rden, s_y1, s_y, s_ytps, s_yT = (sem(n) for n in ("s_den", "s_rden", "s_y1", "s_y", "s_ytps", "s_yT"))
        s_ops, s_r, s_bns, s_mv, s_veps, s_rstd, s_ln = (
            sem(n) for n in ("s_ops", "s_r", "s_bns", "s_mv", "s_veps", "s_rstd", "s_ln"))
        s_x1tps, s_x1Ts, s_lgps, s_lg, s_X1, s_X1T = (
            sem(n) for n in ("s_x1tps", "s_x1Ts", "s_lgps", "s_lg", "s_X1", "s_X1T"))
        s_row = [sem(f"s_row{n}") for n in range(2)]
        s_soft, s_exp, s_score_rows = sem("s_soft"), sem("s_exp"), sem("s_score_rows")
        s_sgps, s_sups, s_sops = sem("s_sgps"), sem("s_sups"), sem("s_sops")
        s_sgg, s_suc, s_hs, s_so, s_acc = (sem(n) for n in ("s_sgg", "s_suc", "s_hs", "s_so", "s_acc"))
        s_accst = [sem(f"s_accst{n}") for n in range(2)]
        s_sT, s_SE, s_cnt, s_tot, s_step, s_thr, s_cand, s_bit = (
            sem(n) for n in ("s_sT", "s_SE", "s_cnt", "s_tot", "s_step", "s_thr", "s_cand", "s_bit"))
        s_pick, s_pickps = sem("s_pick"), sem("s_pickps")
        s_U, s_cps, s_cmp, s_cntt, s_idx = (sem(n) for n in ("s_U", "s_cps", "s_cmp", "s_cntt", "s_idx"))
        s_wt = [sem(f"s_wt{n}") for n in range(2)]
        s_gath = [sem(f"s_gath{n}") for n in range(2)]
        s_scat = [sem(f"s_scat{n}") for n in range(2)]
        s_trps, s_xgT0, s_xgT1 = sem("s_trps"), sem("s_xgT0"), sem("s_xgT1")
        s_ggps, s_uups, s_gg, s_h, s_eops, s_eo = (sem(n) for n in ("s_ggps", "s_uups", "s_gg", "s_h", "s_eops", "s_eo"))
        s_fin = [sem(f"s_fin{n}") for n in range(FG)]
        s_fbns, s_fmv, s_fveps, s_frstd, s_fshift, s_fln, s_out = (
            sem(n) for n in ("s_fbns", "s_fmv", "s_fveps", "s_frstd", "s_fshift", "s_fln", "s_out"))
        NW, NPOOL0, NDVE0 = 11, 6, 12
        NSEARCH = 31

        block = ctx.enter_context(nc.Block())

        @block.sync
        def _(sp):
            def attention(i, par):
                if live(i):
                    wait(sp, s_gps, i - 1)
                    sp.dma_start(xTb[:, par, :], xT[bass.ds(i, 1)].rearrange("o p n -> p (o n)")).then_inc(s_xT[par], 16)
                    wait(sp, s_xb, i - 1)
                    sp.dma_start(xt[:, par], x_tok[:, bass.ds(i * TPB, TPB), :]).then_inc(s_xt[par], 16)
                if isinstance(i, int) and i == 0:
                    for dst, src in ((wkvg_s[:, :], wkvg), (wq_s[:, :], wq), (brow_s[0:1, :], brow), (brow_s[32:33, :], brow),
                                     (cst[:, :], consts), (wo_s[:, :], wo), (bcol[:, :], bcols),
                                     (bo_s[:, :, :], bo.unsqueeze(1).broadcast_to([P, TPB, D])), (gateT_s[:, :], gateT),
                                     (wsgu_s[:, :, :], wsgu), (wsd_s[:, :, :], wsd)):
                        sp.dma_start(dst, src).then_inc(s_w, 16)
                if live(i - 2):
                    wait(sp, s_ln, i - 1)
                    sp.dma_start(rows_tok[:, bass.ds((i - 2) * TPB, TPB), 0:D], x1[:, par]).then_inc(s_row[par], 16)

            sweep(sp, attention, LAG)
            sp.wait_ge(s_soft, 5)
            for g in range(8):
                sp.dma_start(rows_tok.rearrange("p (c g) r -> p g c r", g=8)[:, g, :, D:ROW], S[:, g]).then_inc(s_score_rows, 16)

            def shared(i, par):
                b, q = i - 1, 1 - par
                if live(b):
                    wait(sp, s_acc, b + 1)
                    sp.dma_start(acc_tok[:, bass.ds(b * TPB, TPB), :], so[:, q]).then_inc(s_accst[q], 16)

            sweep(sp, shared, 1)

            def weights(e, par):
                wait(sp, s_eops, (e - 1) * 2)
                sp.dma_start(wgu_s[:, par], wgu[bass.ds(e, 1)].rearrange("o p g i -> p (o g) i")).then_inc(s_wt[par], 16)
                sp.dma_start(wd_s[:, par], wd[bass.ds(e, 1)].rearrange("o p c d -> p (o c) d")).then_inc(s_wt[par], 16)

            for par in range(2):
                sp.wait_ge(s_row[par], 16 * (NB // 2))
            for s in (s_X1, s_X1T, s_lgps, s_y, s_yT):
                sp.wait_ge(s, NB)
            sweep(sp, weights, 0)
            for par in range(2):
                sp.wait_ge(s_scat[par], 16 * ST * (E // 2))

            def load(g, k):
                wait(sp, s_fbns, g - FG + 1)
                sp.dma_start(X1[:, bass.ds(g * FT, FT), :], acc_tok[:, bass.ds(g * FT, FT), :]).then_inc(s_fin[k], 16)

            for k in range(FG):
                load(k, k)
            with sp.Fori(1, NG // FG) as j:
                for k in range(FG):
                    load(j * FG + k, k)
            with sp.Fori(0, NG) as g:
                sp.wait_ge(s_fln, g + 1)
                sp.dma_start(out_tok[:, bass.ds(g * FT, FT), :], X1[:, bass.ds(g * FT, FT), :]).then_inc(s_out, 16)
            sp.wait_ge(s_out, 16 * NG)

        @block.gpsimd
        def _(pool):
            pool.memset(v1[:, 0, :, D:D + 1], 1.0).then_inc(s_pool0, 1)
            pool.memset(v1[:, 1, :, D:D + 1], 1.0).then_inc(s_pool0, 1)
            pool.memset(neghalf[:, :], -0.5).then_inc(s_pool0, 1)
            pool.memset(gprev[:, :], 0.0).then_inc(s_pool0, 1)
            pool.memset(off[:, E:E + 1], 0.0).then_inc(s_pool0, 1)
            pool.wait_ge(s_w, 16 * NW)
            pool.tensor_copy(iota16[:, :], cst[:, C_IOTA:C_END]).then_inc(s_pool0, 1)
            pool.wait_ge(s_pool0, NPOOL0)

            def attention(i, par):
                b, q = i - 1, 1 - par
                if live(i):
                    pool.wait_ge(s_xt[par], landed(i, par))
                    wait(pool, s_r, i - 1)
                    pool.tensor_tensor(xb[:, par], xt[:, par], bo_s[:, :, :], ALU.add).then_inc(s_xb, 1)
                if live(i - 2):
                    wait(pool, s_ln, i - 1)
                    pool.tensor_copy(X1[:, bass.ds((i - 2) * TPB, TPB), :], x1[:, par]).then_inc(s_X1, 1)
                    wait(pool, s_x1Ts, i - 1)
                    pool.tensor_copy(X1T[:, bass.ds((i - 2) * SEQ, SEQ)], x1Ts[:, par]).then_inc(s_X1T, 1)
                if live(b):
                    wait_apart(pool, s_mv, b + 1)
                    pool.tensor_scalar(veps[:, q], mv[:, q, :, 1], LN_EPS, None, ALU.add).then_inc(s_veps, 1)
                    wait(pool, s_veps, b + 1)
                    pool.tensor_tensor(rstd[:, q], veps[:, q], neghalf[:, 0:TPB], ALU.pow).then_inc(s_rstd, 1)

            sweep(pool, attention, LAG)

            def shared(i, par):
                b, q = i - 1, 1 - par
                if live(i):
                    for c in range(SC):
                        wait(pool, s_suc, i * SC + c + 1)
                        wait(pool, s_sops, i - 1)
                        pool.tensor_tensor(hs[:, par, c], sgg[:, c], suc[:, c], ALU.mult).then_inc(s_hs, 1)
                if live(b):
                    wait(pool, s_so, b + 1)
                    pool.tensor_tensor(so[:, q], so[:, q], X1[:, bass.ds(b * TPB, TPB), :], ALU.add).then_inc(s_acc, 1)

            sweep(pool, shared, 1)
            for par in range(2):
                pool.wait_ge(s_row[par], 16 * (NB // 2))
                pool.wait_ge(s_accst[par], 16 * (NB // 2))
            pool.wait_ge(s_score_rows, 16 * 8)

            def routed(i, par):
                b, q = i - 1, 1 - par
                if live(i):
                    wait(pool, s_trps, (i - 1) * 2)
                    wait(pool, s_eo, (i - 1) * 2)
                    wait_apart(pool, s_idx, i + 1)
                    for a in range(ST):
                        pool.indirect_dma_start(out=xg[:, par, a, :], out_offset=None, in_=rows[:, :],
                                                in_offset=bass.IndirectOffsetOnAxis(ap=idx[:, par, a:a + 1], axis=0)
                                                ).then_inc(s_gath[par], 16)
                if live(b):
                    if not (isinstance(b, int) and b == 0):
                        wait_apart(pool, s_scat[par], landed(b - 1, par, ST))
                    for h in range(2):
                        wait_apart(pool, s_eo, b * 2 + h + 1)
                        for a in range(h * HT, h * HT + HT):
                            pool.indirect_dma_start(out=acc[:, :],
                                                    out_offset=bass.IndirectOffsetOnAxis(ap=idxs[:, q, a:a + 1], axis=0),
                                                    in_=eo[:, q, a, :], in_offset=None, compute_op=ALU.add
                                                    ).then_inc(s_scat[q], 16)

            sweep(pool, routed, 1)

            def final(g, p):
                wait(pool, s_fshift, g - 1)
                wait(pool, s_fln, g - 1)
                wait_apart(pool, s_fmv, g + 1)
                pool.tensor_scalar(fveps[:, p], fmv[:, p, :, 1], LN_EPS, None, ALU.add).then_inc(s_fveps, 1)
                wait(pool, s_fveps, g + 1)
                pool.tensor_tensor(frstd[:, p], fveps[:, p], neghalf[:, :], ALU.pow).then_inc(s_frstd, 1)

            for g in range(2):
                final(g, g)
            with pool.Fori(1, NG // 2) as j:
                final(j * 2, 0)
                final(j * 2 + 1, 1)

        @block.scalar
        def _(act):
            act.wait_ge(s_dve0, NDVE0)
            act.wait_ge(s_pool0, NPOOL0)
            act.wait_ge(s_w, 16 * NW)

            def attention(i, par):
                b, q = i - 1, 1 - par
                if live(i):
                    wait(act, s_kps, i + 1)
                    wait(act, s_kf, i - 1)
                    act.activation(nk[:, par], psK[:, :].rearrange("p (t d) -> p t d", d=D), ACT.Relu, scale=-1.0).then_inc(s_nk, 1)
                if live(i - 2):
                    wait(act, s_x1tps, i - 1)
                    wait(act, s_X1T, i - 3)
                    wait(act, s_lgps, i - 3)
                    act.activation(x1Ts[:, par], psOT[:, :], ACT.Copy).then_inc(s_x1Ts, 1)
                if live(i):
                    wait(act, s_nk, i + 1)
                    act.activation(nk[:, par], nk[:, par], ACT.Exp, scale=-1.0).then_inc(s_ek, 1)
                    wait(act, s_vps, i + 1)
                    wait(act, s_kbps, i - 1)
                    act.activation(v1[:, par, :, 0:D], psV[:, :].rearrange("p (t d) -> p t d", d=D), ACT.Copy).then_inc(s_v, 1)
                if live(b):
                    wait(act, s_ytps, b + 1)
                    wait(act, s_ops, b - 1)
                    act.activation(yT[:, q], psYT, ACT.Copy).then_inc(s_yT, 1)
                if live(i):
                    wait(act, s_qps, i + 1)
                    wait(act, s_qf, i - 1)
                    act.activation(nq[:, par], psQ[:, :], ACT.Relu, bias=nqbias[:, :], scale=-1.0).then_inc(s_nq, 1)
                    wait(act, s_nq, i + 1)
                    act.activation(nq[:, par], nq[:, par], ACT.Exp, scale=-1.0).then_inc(s_eq, 1)
                if live(i - 2):
                    wait(act, s_lgps, i - 1)
                    act.activation(LG[:, bass.ds((i - 2) * TPB, TPB), :], kb_lg.rearrange("p (t e) -> p t e", e=E),
                                   ACT.Copy).then_inc(s_lg, 1)
                if live(i):
                    wait(act, s_gps, i + 1)
                    wait(act, s_y, i - 1)
                    act.activation(gate[:, par], psG[:, :].rearrange("p (t d) -> p t d", d=D), ACT.Tanh, scale=0.5).then_inc(s_gate, 1)

            sweep(act, attention, LAG)
            act.wait_ge(s_soft, 2)
            act.activation(LG[:, :, :], LG[:, :, :], ACT.Exp).then_inc(s_exp, 1)

            def shared(i, par):
                b, q = i - 1, 1 - par
                if live(i):
                    for c in range(SC):
                        wait(act, s_sgps, i * SC + c + 1)
                        wait(act, s_hs, (i - 1) * SC + c + 1)
                        act.activation(sgg[:, c], psSG[c][:, :], ACT.Gelu).then_inc(s_sgg, 1)
                        wait(act, s_sups, i * SC + c + 1)
                        act.activation(suc[:, c], psSU[c][:, :], ACT.Copy).then_inc(s_suc, 1)
                if isinstance(i, int) and i == 0:
                    act.wait_ge(s_sT, 1)
                    act.activation(SE[:, :].rearrange("p (h n) -> p h n", h=2), wide[:, :, :], ACT.Copy).then_inc(s_SE, 1)
                if live(b):
                    wait(act, s_sops, b + 1)
                    if not (isinstance(b, int) and b < 2):
                        act.wait_ge(s_accst[q], landed(b - 2, q))
                    act.activation(so[:, q], psSO[:, :].rearrange("p (t d) -> p t d", d=D), ACT.Copy).then_inc(s_so, 1)

            sweep(act, shared, 1)

            def routed(i, par):
                b, q = i - 1, 1 - par
                if live(b):
                    wait(act, s_trps, b * 2 + 1)
                    wait(act, s_uups, b * 2 * IC)
                    act.activation(xgT[:, 0:HALF], psX[0][:, :], ACT.Copy).then_inc(s_xgT0, 1)
                    for k in range(2 * IC):
                        wait(act, s_ggps, b * 2 * IC + k + 1)
                        wait(act, s_h, b * 2 * IC + k - 1)
                        act.activation(gg[:, k % 2], psGG[k % 2][:, :], ACT.Gelu).then_inc(s_gg, 1)

            sweep(act, routed, 1)

            def final(g, p):
                wait(act, s_fshift, g + 1)
                for a in range(FT):
                    v = X1[:, bass.ds(g * FT + a, 1), :].rearrange("p o d -> p (o d)")
                    last = act.activation(v, v, ACT.Identity, bias=fshift[:, p, a:a + 1], scale=frstd[:, p, a:a + 1])
                last.then_inc(s_fln, 1)

            with act.Fori(0, NG // 2) as j:
                final(j * 2, 0)
                final(j * 2 + 1, 1)

        @block.vector
        def _(dve):
            dve.memset(onesraw[:, :], 1.0).then_inc(s_dve0, 1)
            dve.memset(bpair[:, :].bitcast(F32), 0.0).then_inc(s_dve0, 1)
            dve.memset(onespair[:, :].bitcast(F32), 0.0).then_inc(s_dve0, 1)
            dve.wait_ge(s_dve0, 3)
            dve.wait_ge(s_w, 16 * NW)
            for r in (0, 32):
                dve.tensor_copy(onespair[r:r + 1, :], onesraw[r:r + 1, :]).then_inc(s_dve0, 1)
                dve.tensor_copy(bpair[r:r + 1, :], brow_s[r:r + 1, :]).then_inc(s_dve0, 1)
            dve.wait_ge(s_dve0, 7)
            dve.tensor_tensor(bpair[32:33, :], brow_s[32:33, :], bpair[32:33, :].bitcast(F32), ALU.subtract).then_inc(s_dve0, 1)
            dve.tensor_scalar(q1bias[:, :], bcol[:, :], 1.0, None, ALU.add).then_inc(s_dve0, 1)
            dve.tensor_scalar(nqbias[:, :], bcol[:, :], -1.0, None, ALU.mult).then_inc(s_dve0, 1)
            dve.tensor_copy(ident16[:, :], ident).then_inc(s_dve0, 1)
            dve.tensor_copy(diff16[:, :], cst[:, C_DIFF:C_DIFF + P]).then_inc(s_dve0, 1)

            def attention(i, par):
                b, q = i - 1, 1 - par
                if live(b):
                    wait(dve, s_ndps, b + 1)
                    dve.tensor_scalar(den[:, q], kb_den, 2e-6, None, ALU.add).then_inc(s_den, 1)
                    wait(dve, s_den, b + 1)
                    dve.reciprocal(rden[:, q], den[:, q]).then_inc(s_rden, 1)
                if live(i - 2):
                    wait(dve, s_rstd, i - 1)
                    for a in range(TPB):
                        last = dve.tensor_scalar(x1[:, par, a, :], x1[:, par, a, :], mv[:, par, a, 0:1],
                                                 rstd[:, par, a:a + 1], ALU.subtract, ALU.mult)
                    last.then_inc(s_ln, 1)
                if live(b):
                    wait(dve, s_rden, b + 1)
                    zb = rden[:, q].unsqueeze(2).broadcast_to([P, TPB * HEADS, HD])
                    dve.tensor_tensor(y1[:, q].rearrange("p t (h c) -> p (t h) c", c=HD),
                                      psN[:, :].rearrange("p (k c) -> p k c", c=HD), zb, ALU.mult).then_inc(s_y1, 1)
                    wait(dve, s_y1, b + 1)
                    wait(dve, s_gate, b + 1)
                    wait(dve, s_ytps, b - 1)
                    dve.scalar_tensor_tensor(y[:, q], gate[:, q], 1.0, y1[:, q], ALU.add, ALU.mult).then_inc(s_y, 1)
                if live(i):
                    wait(dve, s_ek, i + 1)
                    wait(dve, s_kbps, i - 1)
                    dve.scalar_tensor_tensor(kf[:, par], psK[:, :].rearrange("p (t d) -> p t d", d=D), 1.0, nk[:, par],
                                             ALU.add, ALU.max).then_inc(s_kf, 1)
                    wait(dve, s_eq, i + 1)
                    wait(dve, s_ndps, i - 1)
                    dve.scalar_tensor_tensor(qf[:, par], psQ[:, :], q1bias[:, :], nq[:, par], ALU.add, ALU.max).then_inc(s_qf, 1)
                if live(b):
                    wait(dve, s_ops, b + 1)
                    wait(dve, s_xb, b + 1)
                    if not (isinstance(b, int) and b < 2):
                        dve.wait_ge(s_row[q], landed(b - 2, q))
                    wait(dve, s_X1, b - 1)
                    wait(dve, s_x1tps, b - 1)
                    dve.tensor_tensor(x1[:, q], psOT[:, :].rearrange("p (t d) -> p t d", t=TPB), xb[:, q], ALU.add).then_inc(s_r, 1)
                if live(i):
                    wait(dve, s_kbps, i + 1)
                    wait(dve, s_ndps, i - 1)
                    dve.tensor_tensor(kvbd[:, par], kb_kv[:, 0:D], headmask, ALU.mult).then_inc(s_kvbd, 1)
                    dve.tensor_scalar(ks16[:, par], headsel2, kb_kv[:, D:D + 1], None, ALU.mult).then_inc(s_ks16, 1)
                if live(b):
                    wait(dve, s_r, b + 1)
                    wait(dve, s_mv, b)
                    for a in range(TPB):
                        last = dve.bn_stats(bns[:, a, :], x1[:, q, a, :])
                    last.then_inc(s_bns, 1)
                    wait(dve, s_ln, b - 1)
                    wait_apart(dve, s_bns, b + 1)
                    for a in range(TPB):
                        last = dve.bn_aggr(mv[:, q, a, :], bns[:, a, :])
                    last.then_inc(s_mv, 1)

            sweep(dve, attention, LAG)

            dve.wait_ge(s_lg, NB)
            per_e = [P, NT, E]
            dve.tensor_reduce(stat[:, 0], LG[:, :, :], AX.X, ALU.max).then_inc(s_soft, 1)
            dve.wait_ge(s_soft, 1)
            dve.tensor_tensor(LG[:, :, :], LG[:, :, :], stat[:, 0].unsqueeze(2).broadcast_to(per_e), ALU.subtract).then_inc(s_soft, 1)
            dve.wait_ge(s_exp, 1)
            dve.tensor_reduce(stat[:, 1], LG[:, :, :], AX.X, ALU.add).then_inc(s_soft, 1)
            dve.wait_ge(s_soft, 3)
            dve.reciprocal(stat[:, 2], stat[:, 1]).then_inc(s_soft, 1)
            dve.wait_ge(s_soft, 4)
            for g in range(8):
                tiles = slice(g, NT, 8)
                last = dve.tensor_tensor(S[:, g], LG[:, tiles, :], stat[:, 2, tiles].unsqueeze(2).broadcast_to([P, NT // 8, E]), ALU.mult)
            last.then_inc(s_soft, 1)

            dve.memset(cand[:, :].bitcast(F32), 2.0).then_inc(s_bit, 1)
            dve.memset(thr[:, :].bitcast(F32), 0.0).then_inc(s_bit, 1)
            dve.memset(bitf[:, 1:2], float(2 ** 30)).then_inc(s_bit, 1)
            dve.wait_ge(s_SE, 1)
            dve.wait_ge(s_bit, 3)

            def search(n, par):
                q = 1 - par
                wait(dve, s_cand, n - 1)
                wait(dve, s_thr, n - 1)
                dve.tensor_scalar(junk[:, :], SE[:, :], cand[:, :].bitcast(F32), None, ALU.is_ge, ALU.add,
                                  accum_out=cnt[:, :]).then_inc(s_cnt, 1)
                dve.tensor_scalar(bitf[:, q:q + 1], bitf[:, par:par + 1], 0.5, None, ALU.mult).then_inc(s_bit, 1)
                dve.tensor_scalar(nbit[:, q:q + 1], bitf[:, par:par + 1], 0.5, None, ALU.mult).then_inc(s_bit, 1)
                dve.wait_ge(s_tot, n)
                dve.tensor_scalar(step_i[:, :], psTOT[:, 0:1], float(CAP), bitf[:, par:par + 1], ALU.is_ge, ALU.mult).then_inc(s_step, 1)
                dve.wait_ge(s_bit, n * 2 + 3)
                dve.wait_ge(s_step, n)
                dve.scalar_tensor_tensor(cand[:, :], step_i[:, :], nbit[:, q:q + 1], thr[:, :], ALU.bitwise_or,
                                         ALU.bitwise_or).then_inc(s_cand, 1)
                dve.tensor_tensor(thr[:, :], thr[:, :], step_i[:, :], ALU.bitwise_or).then_inc(s_thr, 1)

            search(1, 1)
            with dve.Fori(1, (NSEARCH + 1) // 2) as j:
                search(j * 2, 0)
                search(j * 2 + 1, 1)
            dve.wait_ge(s_thr, NSEARCH)
            vth = thr[:, :].bitcast(F32)

            dve.tensor_scalar(gtm[:, :], SE[:, :], vth, None, ALU.is_gt, ALU.add, accum_out=tiecnt[:, 0:1]).then_inc(s_pick, 1)
            dve.tensor_scalar(eqm[:, :], SE[:, :], vth, None, ALU.is_equal, ALU.add, accum_out=tiecnt[:, 1:2]).then_inc(s_pick, 1)
            dve.wait_ge(s_pickps, 1)
            dve.tensor_scalar(need[:, :], psTOT[:, 0:1], -1.0, float(CAP), ALU.mult, ALU.add).then_inc(s_pick, 1)
            dve.tensor_copy(tieoff[:, :], psTOT[:, 1:2]).then_inc(s_pick, 1)
            dve.wait_ge(s_pick, 4)
            dve.tensor_tensor_scan(rank[:, :], eqm[:, :], eqm[:, :], tieoff[:, :], ALU.add, ALU.max).then_inc(s_pick, 1)
            dve.wait_ge(s_pick, 5)
            dve.scalar_tensor_tensor(tiesel[:, :], rank[:, :], need[:, :], eqm[:, :], ALU.is_le, ALU.mult).then_inc(s_pick, 1)
            dve.wait_ge(s_pick, 6)
            dve.tensor_tensor(sel[:, :], tiesel[:, :], gtm[:, :], ALU.add).then_inc(s_pick, 1)
            dve.wait_ge(s_pickps, 2)
            selT = psK[:, :].bitcast(F16).rearrange("p (g c e) -> p g c e", g=8, c=8)
            for c in range(8):
                last = dve.tensor_copy(M[:, :, c * 8:c * 8 + 8], selT[:, :, c, :].rearrange("p g e -> p e g"))
            last.then_inc(s_pick, 1)
            dve.wait_ge(s_pick, 8)
            flat = [t[:, :, :].rearrange("p e t -> p (e t)") for t in (M, G)]
            dve.tensor_tensor_scan(flat[1], flat[0], flat[0], 0.0, ALU.add, ALU.max).then_inc(s_pick, 1)
            dve.wait_ge(s_pick, 9)
            dve.tensor_copy(gprev[:, 1:E], G[:, 0:E - 1, NT - 1]).then_inc(s_pick, 1)
            dve.wait_ge(s_pick, 10)
            dve.tensor_tensor(nsel[:, :], G[:, :, NT - 1], gprev[:, :], ALU.subtract).then_inc(s_pick, 1)
            dve.wait_ge(s_pickps, 3)
            dve.tensor_copy(off[:, 0:E], psTOT[:, 0:E]).then_inc(s_pick, 1)
            dve.wait_ge(s_pick, 12)
            dve.tensor_tensor(base[:, :], off[:, 0:E], gprev[:, :], ALU.subtract).then_inc(s_pick, 1)
            dve.wait_ge(s_pick, 13)
            dve.tensor_tensor(C16[:, :, :], G[:, :, :], base[:, :].unsqueeze(2).broadcast_to([P, E, NT]), ALU.add).then_inc(s_pick, 1)
            dve.tensor_copy(tab[:, :, NT], cst[:, C_BLK:C_BLK + E]).then_inc(s_pick, 1)

            def first_slots(e):
                wait_apart(dve, s_cps, e)
                dve.tensor_scalar(U[:, :], iota16[:, :], off[:, bass.ds(e, 1)], None, ALU.is_ge).then_inc(s_U, 1)

            first_slots(0)
            dve.wait_ge(s_pickps, 4)
            for h in range(2):
                last = dve.tensor_copy(tab[:, h * 8:h * 8 + 8, 0:NT], wide[:, h, :].rearrange("p (e t) -> p e t", t=NT))
            last.then_inc(s_pick, 1)

            def routed(i, par):
                b, q = i - 1, 1 - par
                if live(i):
                    cs = wide[:, :, 0:HT * (NT + 1)].rearrange("p h (a t) -> p h a t", t=NT + 1)
                    wait(dve, s_cps, i + 1)
                    wait(dve, s_cntt, i)
                    for h in range(2):
                        last = dve.tensor_tensor(cmp[:, h * HT:h * HT + HT, :], cs[:, h, :, 0:NT],
                                                 slotno[:, h * HT:h * HT + HT].unsqueeze(2).broadcast_to([P, HT, NT]), ALU.is_le)
                    last.then_inc(s_cmp, 1)
                    wait(dve, s_cmp, i + 1)
                    wait(dve, s_idx, i)
                    dve.tensor_reduce(cntt[:, :], cmp[:, :, :], AX.X, ALU.add).then_inc(s_cntt, 1)
                    if not (isinstance(i, int) and i < 2):
                        dve.wait_ge(s_gath[par], landed(i - 2, par, ST))
                    wait(dve, s_cntt, i + 1)
                    dve.scalar_tensor_tensor(idx[:, par].rearrange("p (h a) -> p h a", h=2),
                                             cntt[:, :].rearrange("p (h a) -> p h a", h=2), float(P), cs[:, :, :, NT],
                                             ALU.mult, ALU.add).then_inc(s_idx, 1)
                if live(b):
                    wait(dve, s_trps, b * 2 + 2)
                    wait(dve, s_uups, b * 2 * IC)
                    dve.tensor_copy(xgT[:, HALF:CAP], psX[1][:, :]).then_inc(s_xgT1, 1)
                    for k in range(2 * IC):
                        h, c = k // IC, k % IC
                        wait(dve, s_gg, b * 2 * IC + k + 1)
                        wait(dve, s_uups, b * 2 * IC + k + 1)
                        wait(dve, s_eops, b * 2 - 1 + h)
                        dve.tensor_tensor(hT[:, c, h * HALF:(h + 1) * HALF], gg[:, k % 2], psUU[k % 2][:, :], ALU.mult).then_inc(s_h, 1)
                if live(i):
                    first_slots(i + 1)
                if live(b):
                    for h in range(2):
                        wait(dve, s_eops, b * 2 + h + 1)
                        if h == 0 and not (isinstance(b, int) and b < 2):
                            dve.wait_ge(s_scat[q], landed(b - 2, q, ST))
                        if h == 0:
                            wait_apart(dve, s_idx, b + 1)
                            dve.tensor_copy(idxs[:, q], idx[:, q])
                        w = xg[:, q, h * HT:h * HT + HT, bass.ds(b + D, 1)].broadcast_to([P, HT, D])
                        dve.tensor_tensor(eo[:, q, h * HT:h * HT + HT, :], psX[h][:, :].rearrange("p (a d) -> p a d", d=D), w,
                                          ALU.mult).then_inc(s_eo, 1)

            sweep(dve, routed, 1)

            def final(g, k):
                p = k % 2
                dve.wait_ge(s_fin[k], 16 * (g // FG + 1) if isinstance(g, int) else (g - k) * 4 + 16)
                wait(dve, s_fmv, g)
                for a in range(FT):
                    last = dve.bn_stats(fbns[:, a, :], X1[:, bass.ds(g * FT + a, 1), :].rearrange("p o d -> p (o d)"))
                last.then_inc(s_fbns, 1)
                wait(dve, s_fshift, g - 1)
                wait_apart(dve, s_fbns, g + 1)
                for a in range(FT):
                    last = dve.bn_aggr(fmv[:, p, a, :], fbns[:, a, :])
                last.then_inc(s_fmv, 1)

            def shift(g, k):
                p = k % 2
                wait(dve, s_frstd, g + 1)
                wait(dve, s_fln, g - 1)
                dve.scalar_tensor_tensor(fshift[:, p], fmv[:, p, :, 0], -1.0, frstd[:, p], ALU.mult, ALU.mult).then_inc(s_fshift, 1)

            for k in range(FG):
                final(k, k)
                if k:
                    shift(k - 1, k - 1)
            with dve.Fori(1, NG // FG) as j:
                for k in range(FG):
                    final(j * FG + k, k)
                    shift(j * FG + k - 1, (k - 1) % FG)
            shift(NG - 1, FG - 1)

        @block.tensor
        def _(pe):
            pe.wait_ge(s_w, 16 * NW)
            pe.wait_ge(s_dve0, NDVE0)
            pe.wait_ge(s_pool0, NPOOL0)

            def project(ps, par, n):
                for a in range(TPB):
                    pe.matmul(ps[:, a * D:(a + 1) * D], onespair[:, :], bpair[:, n * D:(n + 1) * D], start=True, stop=False)
                    last = pe.matmul(ps[:, a * D:(a + 1) * D], xTb[:, par, a * P:(a + 1) * P], wkvg_s[:, n * D:(n + 1) * D],
                                     start=False, stop=True)
                return last

            def attention(i, par):
                b, q = i - 1, 1 - par
                if live(i):
                    pe.wait_ge(s_xT[par], landed(i, par))
                    wait(pe, s_kf, i)
                    project(psK, par, 0).then_inc(s_kps, 1)
                if live(i - 2):
                    wait(pe, s_ln, i - 1)
                    wait(pe, s_r, i - 1)
                    for a in range(TPB):
                        last = pe.transpose(psOT[:, a * P:(a + 1) * P], x1[:, par, a, :], ident)
                    last.then_inc(s_x1tps, 1)
                if live(i):
                    wait(pe, s_v, i)
                    project(psV, par, 1).then_inc(s_vps, 1)
                if live(b):
                    wait(pe, s_y, b + 1)
                    wait(pe, s_yT, b)
                    for a in range(TPB):
                        last = pe.transpose(psYT[:, a * P:(a + 1) * P], y[:, q, a, :], ident)
                    last.then_inc(s_ytps, 1)
                if live(i):
                    wait(pe, s_qf, i)
                    pe.matmul(psQ[:, :], wq_s[:, :], xTb[:, par], start=True, stop=True).then_inc(s_qps, 1)
                if live(i - 2):
                    wait(pe, s_x1Ts, i - 1)
                    wait(pe, s_den, b)
                    for a in range(TPB):
                        last = pe.matmul(kb_lg[:, a * E:(a + 1) * E], x1Ts[:, par, a * P:(a + 1) * P], gateT_s[:, :], start=True, stop=True)
                    last.then_inc(s_lgps, 1)
                if live(i):
                    wait(pe, s_gate, i)
                    project(psG, par, 2).then_inc(s_gps, 1)
                if live(b):
                    wait(pe, s_yT, b + 1)
                    wait(pe, s_x1Ts, b - 1)
                    for a in range(TPB):
                        last = pe.matmul(psOT[:, a * D:(a + 1) * D], yT[:, q, a * P:(a + 1) * P], wo_s[:, :], start=True, stop=True)
                    last.then_inc(s_ops, 1)
                if live(i):
                    wait(pe, s_kf, i + 1)
                    wait(pe, s_v, i + 1)
                    wait(pe, s_den, i)
                    wait(pe, s_lg, i - 1)
                    for a in range(TPB):
                        last = pe.matmul(kb_kv, kf[:, par, a, :], v1[:, par, a, :], start=(a == 0), stop=(a == TPB - 1))
                    last.then_inc(s_kbps, 1)
                    wait(pe, s_ks16, i + 1)
                    wait(pe, s_kvbd, i + 1)
                    wait(pe, s_qf, i + 1)
                    wait(pe, s_y1, i)
                    for a in range(TPB):
                        pe.matmul(kb_den[:, a * HEADS:(a + 1) * HEADS], qf[:, par, a * P:(a + 1) * P], ks16[:, par], start=True, stop=True)
                        last = pe.matmul(psN[:, a * D:(a + 1) * D], qf[:, par, a * P:(a + 1) * P], kvbd[:, par], start=True, stop=True)
                    last.then_inc(s_ndps, 1)

            sweep(pe, attention, LAG)
            for s in (s_kf, s_v, s_gate, s_qf, s_yT, s_y1, s_r, s_x1Ts, s_lg, s_den):
                pe.wait_ge(s, NB)

            def count(n):
                wait(pe, s_cnt, n)
                pe.matmul(psTOT[:, 0:1], same_expert, cnt[:, :], start=True, stop=True).then_inc(s_tot, 1)

            def shared(i, par):
                b, q = i - 1, 1 - par
                if live(i):
                    wait(pe, s_X1T, i + 1)
                    for c in range(SC):
                        wait(pe, s_sgg, i * SC + c - 1)
                        pe.matmul(psSG[c][:, :], wsgu_s[:, 0, c * P:(c + 1) * P], X1T[:, bass.ds(i * SEQ, SEQ)],
                                  start=True, stop=True).then_inc(s_sgps, 1)
                        wait(pe, s_suc, i * SC + c - 1)
                        pe.matmul(psSU[c][:, :], wsgu_s[:, 1, c * P:(c + 1) * P], X1T[:, bass.ds(i * SEQ, SEQ)],
                                  start=True, stop=True).then_inc(s_sups, 1)
                        if isinstance(i, int) and i == 0:
                            if c == 1:
                                pe.wait_ge(s_soft, 5)
                                for g in range(8):
                                    last = pe.transpose(wide[:, g // 4, g % 4 * P:(g % 4 + 1) * P], S[:, g].rearrange("p c e -> p (c e)"), ident)
                                last.then_inc(s_sT, 1)
                                count(1)
                        else:
                            count(i * 2 + c)
                if live(b):
                    wait(pe, s_hs, b * SC + SC)
                    wait(pe, s_so, b)
                    for a in range(TPB):
                        for c in range(SC):
                            last = pe.matmul(psSO[:, a * D:(a + 1) * D], hs[:, q, c, a * P:(a + 1) * P], wsd_s[:, c, :],
                                             start=(c == 0), stop=(c == SC - 1))
                    last.then_inc(s_sops, 1)

            sweep(pe, shared, 1)
            pe.wait_ge(s_pick, 2)
            pe.matmul(psTOT[:, 0:1], same_expert, tiecnt[:, 0:1], start=True, stop=True)
            pe.matmul(psTOT[:, 1:2], earlier_run, tiecnt[:, 1:2], start=True, stop=True).then_inc(s_pickps, 1)
            pe.wait_ge(s_pick, 7)
            pe.wait_ge(s_sgg, NB * SC)
            for g in range(8):
                last = pe.transpose(psK[:, :].bitcast(F16)[:, g * P:(g + 1) * P], sel[:, g * P:(g + 1) * P], ident16[:, :])
            last.then_inc(s_pickps, 1)
            pe.wait_ge(s_pick, 11)
            pe.matmul(psTOT[:, 0:E], upper, nsel[:, :], start=True, stop=True).then_inc(s_pickps, 1)
            pe.wait_ge(s_pick, 15)
            pe.wait_ge(s_SE, 1)
            for h in range(2):
                last = pe.matmul(wide[:, h, :], diff16[:, :], C16[:, h * 8:h * 8 + 8, :].rearrange("p e t -> p (e t)"), start=True, stop=True)
            last.then_inc(s_pickps, 1)
            for s, n in ((s_sgg, SC), (s_suc, SC), (s_so, 1)):
                pe.wait_ge(s, NB * n)
            pe.wait_ge(s_pick, 16)

            def routed(i, par):
                b, q = i - 1, 1 - par
                if live(b):
                    pe.wait_ge(s_gath[q], landed(b, q, ST))
                    wait(pe, s_eo, b * 2 - 1)
                    for a in range(HT):
                        last = pe.transpose(psX[0][:, a * P:(a + 1) * P], xg[:, q, a, 0:D], ident)
                    last.then_inc(s_trps, 1)
                if live(i):
                    wait(pe, s_U, i + 1)
                    wait(pe, s_idx, i)
                    for a in range(ST):
                        last = pe.matmul(wide[:, a // HT, a % HT * (NT + 1):(a % HT + 1) * (NT + 1)], U[:, a * P:(a + 1) * P],
                                         tab[:, bass.ds(i, 1), :].rearrange("p o t -> p (o t)"), start=True, stop=True)
                    last.then_inc(s_cps, 1)
                if live(b):
                    wait(pe, s_eo, b * 2)
                    for a in range(HT, ST):
                        last = pe.transpose(psX[1][:, (a - HT) * P:(a - HT + 1) * P], xg[:, q, a, 0:D], ident)
                    last.then_inc(s_trps, 1)
                    pe.wait_ge(s_wt[q], landed(b, q, 2))
                    for h in range(2):
                        wait(pe, (s_xgT0, s_xgT1)[h], b + 1)
                        for c in range(IC):
                            k = h * IC + c
                            wait(pe, s_gg, b * 2 * IC + k - 1)
                            wait(pe, s_h, b * 2 * IC + k - 1)
                            pe.matmul(psGG[k % 2][:, :], wgu_s[:, q, 0, c * P:(c + 1) * P], xgT[:, h * HALF:(h + 1) * HALF],
                                      start=True, stop=True).then_inc(s_ggps, 1)
                            pe.matmul(psUU[k % 2][:, :], wgu_s[:, q, 1, c * P:(c + 1) * P], xgT[:, h * HALF:(h + 1) * HALF],
                                      start=True, stop=True).then_inc(s_uups, 1)
                    for h in range(2):
                        wait(pe, s_h, b * 2 * IC + (h + 1) * IC)
                        for a in range(HT):
                            for c in range(IC):
                                last = pe.matmul(psX[h][:, a * D:(a + 1) * D], hT[:, c, h * HALF + a * P:h * HALF + (a + 1) * P],
                                                 wd_s[:, q, c, :], start=(c == 0), stop=(c == IC - 1))
                        last.then_inc(s_eops, 1)

            sweep(pe, routed, 1)


def kernel(**inputs):
    import concourse.bacc as bacc
    from concourse.bass_utils import run_bass_kernel_spmd

    g = {k: np.ascontiguousarray(v) for k, v in inputs.items()}
    arrays = {
        "x": g["L0_attn_x"],
        "xT": g["L0_attn_x"].transpose(0, 2, 1),
        "wq": g["L0_attn_wq_w"],
        "wkvg": np.concatenate([g["L0_attn_wk_w"], g["L0_attn_wv_w"], g["L0_attn_wg_w"]], axis=1),
        "wo": g["L0_attn_out_w"],
        "bcols": g["L0_attn_wq_b"][:, None],
        "brow": np.concatenate([g["L0_attn_wk_b"], g["L0_attn_wv_b"], g["L0_attn_wg_b"]])[None, :],
        "bo": np.broadcast_to(g["L0_attn_out_b"][None, :], (P, D)),
        "consts": constants(),
        "gateT": g["L0_ffn_gate_w"].T,
        "wsgu": np.stack([g["L0_ffn_Sg"].T, g["L0_ffn_Su"].T], axis=1),
        "wsd": g["L0_ffn_Sd"].T.reshape(SC, P, D).transpose(1, 0, 2),
        "wgu": np.stack([g["L0_ffn_Wg"].transpose(0, 2, 1), g["L0_ffn_Wu"].transpose(0, 2, 1)], axis=2),
        "wd": g["L0_ffn_Wd"].transpose(0, 2, 1).reshape(E, IC, P, D).transpose(0, 2, 1, 3),
    }
    arrays = {f"in_{n}": np.ascontiguousarray(a) for n, a in arrays.items()}
    nc = bacc.Bacc("TRN2", target_bir_lowering=False, num_devices=1)
    args = [nc.dram_tensor(n, a.shape, mybir.dt.from_np(a.dtype), kind="ExternalInput").ap() for n, a in arrays.items()]
    args.append(nc.dram_tensor("out", (NB, SEQ, D), F32, kind="ExternalOutput").ap())
    program(nc, *args)
    r = run_bass_kernel_spmd(nc, [arrays], core_ids=[0])
    return r.results[0]["out"]
```

```python
from contextlib import ExitStack

import numpy as np

import concourse.bass as bass
from concourse import mybir

F32 = mybir.dt.float32
F32R = mybir.dt.float32r
F16 = mybir.dt.float16
U16 = mybir.dt.uint16
I32 = mybir.dt.int32
ACT = mybir.ActivationFunctionType
ALU = mybir.AluOpType
AX = mybir.AxisListType

P = 128
D = 128
HEADS = 16
HD = D // HEADS
NB = 16
SEQ = 512
TPB = SEQ // P
T = NB * SEQ
NT = T // P
E = 16
CAP = 2 * T // E
ST = CAP // P
HALF = CAP // 2
HT = ST // 2
I = 512
IC = I // P
SC = 2
ROW = D + E
NC = NT // 8
LN_EPS = 1e-5
WEIGHTS_AT = (0, 4, 6)
LAG = 2
FT = 8
NG = NT // FT
FG = 4

C_IDENT, C_HEAD, C_SAME, C_PREF, C_UPPER, C_DIFF, C_SEL2, C_SLOT, C_BLK, C_END = np.cumsum(
    [0, P, P, P, P, P, P, HEADS, ST, E]).tolist()


def constants():
    c = np.zeros((P, C_END), np.float32)
    r, q = np.arange(P)[:, None], np.arange(P)[None, :]
    c[:, C_IDENT:C_IDENT + P] = r == q
    c[:, C_HEAD:C_HEAD + P] = r // HD == q // HD
    c[:, C_SAME:C_SAME + P] = r % E == q % E
    c[:, C_PREF:C_PREF + P] = (r % E == q % E) & (r // E < q // E)
    c[:, C_UPPER:C_UPPER + P] = r < q
    c[:, C_DIFF:C_DIFF + P] = (r == q) * 1.0 - (r == q - 1) * 1.0
    c[:, C_SEL2:C_SEL2 + HEADS] = 2.0 * (r // HD == np.arange(HEADS)[None, :])
    c[:, C_SLOT:C_SLOT + ST] = r + P * np.arange(ST)[None, :]
    c[:, C_BLK:C_BLK + E] = r >= 1
    return c


def program(nc, x, xT, wq, wkvg, wo, bcols, brow, bo, consts, iota, gateT, wsgu, wsd, wgu, wd, out):
    with ExitStack() as ctx:
        def sb(name, shape, dt=F32):
            return ctx.enter_context(nc.sbuf_tensor(name, shape, dt))

        def region(name, size):
            whole = sb(name, [P, size])

            def layout():
                at = [0]

                def carve(shape, dt=F32):
                    n = int(np.prod(shape[1:]))
                    assert at[0] + n <= size
                    part = whole[:, at[0]:at[0] + n]
                    at[0] += n
                    if dt != F32:
                        part = part.bitcast(dt)
                    dims = "abcd"[:len(shape) - 1]
                    sizes = dict(zip(dims, shape[1:]))
                    return part.rearrange(f"p ({' '.join(dims)}) -> p {' '.join(dims)}", **sizes)

                return carve

            return layout

        def sem(name):
            return ctx.enter_context(nc.semaphore(name))

        def wait(eng, s, v):
            if not (isinstance(v, int) and v <= 0):
                eng.wait_ge(s, v)

        def wait_apart(eng, s, v):
            wait(eng, s, v)
            if not isinstance(v, int):
                eng.sem_inc(s_apart, 1)

        def landed(i, par, ndma=1):
            return 16 * ndma * (i // 2 + 1) if isinstance(i, int) else (i - par) * (8 * ndma) + 16 * ndma

        def live(b, n=NB):
            return not isinstance(b, int) or 0 <= b < n

        def sweep(eng, step, lag, peel=4, first=0, stop=NB):
            for i in range(first, peel):
                step(i, i % 2)
            with eng.Fori(peel // 2, stop // 2) as j:
                step(j * 2, 0)
                step(j * 2 + 1, 1)
            for i in range(stop, stop + lag):
                step(i, i % 2)

        rows = nc.dram_tensor("rows", [T, ROW], F32, kind="Internal").ap()
        acc = nc.dram_tensor("acc", [T, D], F32, kind="Internal").ap()
        rows_tok = rows.rearrange("(t p) r -> p t r", p=P)
        acc_tok = acc.rearrange("(t p) d -> p t d", p=P)
        x_tok = x.rearrange("b (t p) d -> p (b t) d", p=P)
        out_tok = out.rearrange("b (t p) d -> p (b t) d", p=P)

        cst = sb("cst", [P, C_END])
        ident = cst[:, C_IDENT:C_IDENT + P]
        headmask = cst[:, C_HEAD:C_HEAD + P]
        same_expert = cst[:, C_SAME:C_SAME + P]
        earlier_run = cst[:, C_PREF:C_PREF + P]
        upper = cst[:, C_UPPER:C_UPPER + P]
        headsel2 = cst[:, C_SEL2:C_SEL2 + HEADS]
        slotno = cst[:, C_SLOT:C_SLOT + ST]
        ident16 = sb("ident16", [P, P], F16)
        diff16 = sb("diff16", [P, P], F16)
        iota16 = sb("iota16", [P, CAP], F16)
        wq_s, wo_s = sb("wq_s", [P, D]), sb("wo_s", [P, D])
        wkvg_s = sb("wkvg_s", [P, 3 * D])
        bcol = sb("bcol", [P, 1])
        q1bias, nqbias = sb("q1bias", [P, 1]), sb("nqbias", [P, 1])
        bpair = sb("bpair", [33, 3, TPB * D], F32R)
        onespair = sb("onespair", [33, P], F32R)
        bo_s = sb("bo_s", [P, TPB, D])
        neghalf = sb("neghalf", [P, FT])
        gateT_s = sb("gateT_s", [P, E])
        wsgu_s = sb("wsgu_s", [P, 2, SC * P])
        wsd_s = sb("wsd_s", [P, SC, D])

        work = region("work", 16640)
        at = work()
        xTb = at([P, 2, SEQ])
        xt, xb, x1 = (at([P, 2, TPB, D]) for _ in range(3))
        x1Ts = at([P, 2, SEQ])
        nk, kf, gate = (at([P, 2, TPB, D]) for _ in range(3))
        v1 = at([P, 2, TPB, D + 1])
        nq, qf = at([P, 2, SEQ]), at([P, 2, SEQ])
        kvks = at([P, 2, D + HEADS])
        den, rden = at([P, 2, TPB, HEADS]), at([P, 2, TPB, HEADS])
        y1, y = at([P, 2, TPB, D]), at([P, 2, TPB, D])
        yT = at([P, 2, SEQ])
        bns = at([P, TPB, 6])
        mv = at([P, 2, TPB, 2])
        veps, rstd = at([P, 2, TPB]), at([P, 2, TPB])

        LG = sb("LG", [P, NT, E])
        S = sb("S", [P, 8, NT // 8, E])
        SE = sb("SE", [P, CAP])
        stat = sb("stat", [P, 3, NT])
        top = sb("top", [P, CAP], U16)
        rest = sb("rest", [P, CAP], U16)
        junk = sb("junk", [P, CAP], F16)
        cnt, cand, step, quota, thrf = (sb(n, [P, 1]) for n in ("cnt", "cand", "step", "quota", "thrf"))
        bit = sb("bit", [P, 2])
        thr_top, thr_rest, thr = (sb(n, [P, 1], I32) for n in ("thr_top", "thr_rest", "thr"))
        tiecnt = sb("tiecnt", [P, 2])
        need, tieoff = sb("need", [P, 1]), sb("tieoff", [P, 1])
        gtm, eqm, tiesel, sel = (sb(n, [P, CAP], F16) for n in ("gtm", "eqm", "tiesel", "sel"))
        rank = sb("rank", [P, CAP])
        M = sb("M", [P, E, NT])
        G = sb("G", [P, E, NT])
        gprev, nsel, base = (sb(n, [P, E]) for n in ("gprev", "nsel", "base"))
        off = sb("off", [P, E + 1])
        C16 = sb("C16", [P, E, NT], F16)
        tab = sb("tab", [P, E, NT + 1], F16)
        U = sb("U", [P, CAP], F16)

        cmp = sb("cmp", [P, ST, NT])
        cntt = sb("cntt", [P, ST])
        idx = sb("idx", [P, 2, ST], I32)
        idxs = sb("idxs", [P, 2, ST], I32)
        at = work()
        xg = at([P, 2, ST, ROW])
        wgu_s = at([P, 2, 2, I])
        wd_s = at([P, 2, IC, D])
        sgg, suc = at([P, SC, SEQ]), at([P, SC, SEQ])
        hs = at([P, 2, SC, SEQ])
        so = at([P, 2, TPB, D])
        gg, hraw = at([P, 2, HALF]), at([P, 2, HALF])
        eoT = at([P, 2, HALF])
        score = at([P, 2, ST])
        eo = at([P, 2, ST, D])
        at = work()
        fbns, fmv = at([P, FT, 6]), at([P, 2, FT, 2])
        fveps, frstd, fshift = (at([P, 2, FT]) for _ in range(3))

        with nc.sbuf_tensor("X1", [P, NT, D], F32) as X1, nc.sbuf_tensor("X1T", [P, T], F32) as X1T:
            pass
        brow_s = X1T
        hTh, hTl = sb("hTh", [P, IC, CAP], F32R), sb("hTl", [P, IC, CAP], F32R)
        wguh, wgul = sb("wguh", [P, 2, 2, I], F32R), sb("wgul", [P, 2, 2, I], F32R)
        wdh, wdl = sb("wdh", [P, 2, IC, D], F32R), sb("wdl", [P, 2, IC, D], F32R)
        xgTh, xgTl = sb("xgTh", [P, CAP], F32R), sb("xgTl", [P, CAP], F32R)

        bank = [ctx.enter_context(nc.psum_tensor(f"bank{n}", [P, 512], F32)) for n in range(6)]
        wide = ctx.enter_context(nc.psum_tensor("wide", [P, 2, 512], F32))
        psK, psV, psG, psQ, psN, psOT = bank
        psYT, psKB = wide[:, 0, :], wide[:, 1, :]
        ND = D + HEADS
        kb_kv, kb_nd, kb_lg = psKB[:, 0:D + 1], psKB[:, ND:2 * ND], psKB[:, 2 * ND:2 * ND + TPB * E]
        psN3 = psN[:, 0:(TPB - 1) * ND].rearrange("p (t n) -> p t n", n=ND)
        psSG, psSU, psSO, psTOT = bank[0:2], bank[2:4], bank[4], bank[5]
        psX, psGG, psUU = bank[0:2], bank[2:4], bank[4:6]
        psXT = psGG

        s_apart, s_pool0, s_dve0, s_bhi, s_blo, s_qb = (sem(n) for n in ("s_apart", "s_pool0", "s_dve0", "s_bhi", "s_blo", "s_qb"))
        s_wproj, s_wattn, s_wlater, s_iota, s_cast = (sem(n) for n in ("s_wproj", "s_wattn", "s_wlater", "s_iota", "s_cast"))
        s_xT = [sem(f"s_xT{n}") for n in range(2)]
        s_xt = [sem(f"s_xt{n}") for n in range(2)]
        s_kps, s_vps, s_qps, s_gps = (sem(n) for n in ("s_kps", "s_vps", "s_qps", "s_gps"))
        s_nk, s_ek, s_v, s_nq, s_eq, s_gate = (sem(n) for n in ("s_nk", "s_ek", "s_v", "s_nq", "s_eq", "s_gate"))
        s_kf, s_qf, s_xb = sem("s_kf"), sem("s_qf"), sem("s_xb")
        s_kbps, s_kvks, s_ndps = (sem(n) for n in ("s_kbps", "s_kvks", "s_ndps"))
        s_den, s_rden, s_y1, s_y, s_ytps, s_yT = (sem(n) for n in ("s_den", "s_rden", "s_y1", "s_y", "s_ytps", "s_yT"))
        s_ops, s_r, s_bns, s_mv, s_veps, s_rstd, s_ln = (
            sem(n) for n in ("s_ops", "s_r", "s_bns", "s_mv", "s_veps", "s_rstd", "s_ln"))
        s_x1tps, s_x1Ts, s_lgps, s_lg, s_X1, s_X1T = (
            sem(n) for n in ("s_x1tps", "s_x1Ts", "s_lgps", "s_lg", "s_X1", "s_X1T"))
        s_row = [sem(f"s_row{n}") for n in range(2)]
        s_soft, s_exp, s_score_rows = sem("s_soft"), sem("s_exp"), sem("s_score_rows")
        s_sgps, s_sups, s_sops = sem("s_sgps"), sem("s_sups"), sem("s_sops")
        s_sgg, s_suc, s_hs, s_so, s_acc = (sem(n) for n in ("s_sgg", "s_suc", "s_hs", "s_so", "s_acc"))
        s_accst = [sem(f"s_accst{n}") for n in range(2)]
        s_sT, s_SE, s_cnt, s_tot, s_step, s_thr, s_cand, s_bit, s_top, s_quota = (
            sem(n) for n in ("s_sT", "s_SE", "s_cnt", "s_tot", "s_step", "s_thr", "s_cand", "s_bit", "s_top", "s_quota"))
        s_pick, s_pickps = sem("s_pick"), sem("s_pickps")
        s_U, s_cps, s_cmp, s_cntt, s_idx = (sem(n) for n in ("s_U", "s_cps", "s_cmp", "s_cntt", "s_idx"))
        s_wt = [sem(f"s_wt{n}") for n in range(2)]
        s_gath = [[sem(f"s_gath{n}{h}") for h in range(2)] for n in range(2)]
        s_scat = [sem(f"s_scat{n}") for n in range(2)]
        s_trps, s_xhi, s_xlo, s_whi, s_wlo, s_idxs, s_score, s_eoT, s_backps = (
            sem(n) for n in ("s_trps", "s_xhi", "s_xlo", "s_whi", "s_wlo", "s_idxs", "s_score", "s_eoT", "s_backps"))
        s_ggps, s_uups, s_gg, s_h, s_hhi, s_hlo, s_eops, s_eo = (
            sem(n) for n in ("s_ggps", "s_uups", "s_gg", "s_h", "s_hhi", "s_hlo", "s_eops", "s_eo"))
        s_fin = [sem(f"s_fin{n}") for n in range(FG)]
        s_fbns, s_fmv, s_fveps, s_frstd, s_fshift, s_flast, s_fln, s_out = (
            sem(n) for n in ("s_fbns", "s_fmv", "s_fveps", "s_frstd", "s_fshift", "s_flast", "s_fln", "s_out"))
        NPROJ, NATTN, NLATER = 5, 4, 3
        NPOOL0, NDVE0 = 5, 4
        NTOP, NREST = 14, 16
        NCOUNT = NTOP + 1 + NREST

        block = ctx.enter_context(nc.Block())

        @block.sync
        def _(sp):
            def attention(i, par):
                if live(i):
                    wait(sp, s_gps, i - 1)
                    sp.dma_start(xTb[:, par, :], xT[bass.ds(i, 1)].rearrange("o p n -> p (o n)")).then_inc(s_xT[par], 16)
                    wait(sp, s_xb, i - 1)
                    sp.dma_start(xt[:, par], x_tok[:, bass.ds(i * TPB, TPB), :]).then_inc(s_xt[par], 16)
                if isinstance(i, int) and i == 0:
                    for dst, src in ((cst[:, :], consts), (bo_s[:, :, :], bo.unsqueeze(1).broadcast_to([P, TPB, D])),
                                     (wo_s[:, :], wo), (gateT_s[:, :], gateT)):
                        sp.dma_start(dst, src).then_inc(s_wattn, 16)
                    for dst, src in ((SE[:, :], iota), (wsgu_s[:, :, :], wsgu), (wsd_s[:, :, :], wsd)):
                        sp.dma_start(dst, src).then_inc(s_wlater, 16)
                if live(i - 2):
                    wait(sp, s_ln, i - 1)
                    sp.dma_start(rows_tok[:, bass.ds((i - 2) * TPB, TPB), 0:D], x1[:, par]).then_inc(s_row[par], 16)

            sp.dma_start(wkvg_s[:, :], wkvg).then_inc(s_wproj, 16)
            sweep(sp, attention, LAG)
            def weights(e, par):
                wait(sp, s_wlo, (e - 1) * 3)
                sp.dma_start(wgu_s[:, par], wgu[bass.ds(e, 1)].rearrange("o p g i -> p (o g) i")).then_inc(s_wt[par], 16)
                sp.dma_start(wd_s[:, par], wd[bass.ds(e, 1)].rearrange("o p c d -> p (o c) d")).then_inc(s_wt[par], 16)

            for par in range(2):
                sp.wait_ge(s_row[par], 16 * (NB // 2))
            for s in (s_X1, s_X1T, s_lgps, s_y, s_yT):
                sp.wait_ge(s, NB)
            for e in range(2):
                weights(e, e)
            sp.wait_ge(s_soft, 5)
            for g in range(8):
                sp.dma_start(rows_tok.rearrange("p (c g) r -> p g c r", g=8)[:, g, :, D:ROW], S[:, g]).then_inc(s_score_rows, 16)

            def shared(i, par):
                b, q = i - 1, 1 - par
                if live(b):
                    wait(sp, s_acc, b + 1)
                    sp.dma_start(acc_tok[:, bass.ds(b * TPB, TPB), :], so[:, q]).then_inc(s_accst[q], 16)

            sweep(sp, shared, 1)

            sweep(sp, weights, 0, first=2)
            for par in range(2):
                sp.wait_ge(s_scat[par], 16 * ST * (E // 2))

            def load(g, k):
                wait(sp, s_fbns, g - FG + 1)
                sp.dma_start(X1[:, bass.ds(g * FT, FT), :], acc_tok[:, bass.ds(g * FT, FT), :]).then_inc(s_fin[k], 16)

            for k in range(FG):
                load(k, k)
            with sp.Fori(1, NG // FG) as j:
                for k in range(FG):
                    load(j * FG + k, k)
            with sp.Fori(0, NG) as g:
                sp.wait_ge(s_fln, g + 1)
                sp.wait_ge(s_flast, g + 1)
                sp.dma_start(out_tok[:, bass.ds(g * FT, FT), :], X1[:, bass.ds(g * FT, FT), :]).then_inc(s_out, 16)
            sp.wait_ge(s_out, 16 * NG)

        @block.gpsimd
        def _(pool):
            pool.memset(v1[:, 0, :, D:D + 1], 1.0).then_inc(s_pool0, 1)
            pool.memset(v1[:, 1, :, D:D + 1], 1.0).then_inc(s_pool0, 1)
            pool.memset(neghalf[:, :], -0.5).then_inc(s_pool0, 1)
            pool.memset(gprev[:, :], 0.0).then_inc(s_pool0, 1)
            pool.memset(off[:, E:E + 1], 0.0).then_inc(s_pool0, 1)
            pool.wait_ge(s_pool0, NPOOL0)
            pool.wait_ge(s_wattn, 16 * NATTN)

            def attention(i, par):
                b, q = i - 1, 1 - par
                if live(i):
                    pool.wait_ge(s_xt[par], landed(i, par))
                    wait(pool, s_r, i - 1)
                    pool.tensor_tensor(xb[:, par], xt[:, par], bo_s[:, :, :], ALU.add).then_inc(s_xb, 1)
                if live(i - 2):
                    wait(pool, s_ln, i - 1)
                    pool.tensor_copy(X1[:, bass.ds((i - 2) * TPB, TPB), :], x1[:, par]).then_inc(s_X1, 1)
                if live(b):
                    wait_apart(pool, s_mv, b + 1)
                    pool.tensor_scalar(veps[:, q], mv[:, q, :, 1], LN_EPS, None, ALU.add).then_inc(s_veps, 1)
                    wait(pool, s_veps, b + 1)
                    pool.tensor_tensor(rstd[:, q], veps[:, q], neghalf[:, 0:TPB], ALU.pow).then_inc(s_rstd, 1)

            sweep(pool, attention, LAG)

            def shared(i, par):
                b, q = i - 1, 1 - par
                if live(i):
                    for c in range(SC):
                        wait(pool, s_suc, i * SC + c + 1)
                        wait(pool, s_sops, i - 1)
                        pool.tensor_tensor(hs[:, par, c], sgg[:, c], suc[:, c], ALU.mult).then_inc(s_hs, 1)
                if live(b):
                    wait(pool, s_so, b + 1)
                    pool.tensor_tensor(so[:, q], so[:, q], X1[:, bass.ds(b * TPB, TPB), :], ALU.add).then_inc(s_acc, 1)

            sweep(pool, shared, 1, stop=NB - 2)
            for par in range(2):
                pool.wait_ge(s_row[par], 16 * (NB // 2))
            pool.wait_ge(s_score_rows, 16 * 8)

            def routed(i, par):
                b, d, q = i - 4, i - 1, 1 - par
                if live(b):
                    if isinstance(b, int) and b == 0:
                        for n in range(2):
                            pool.wait_ge(s_accst[n], 16 * (NB // 2))
                    if not (isinstance(b, int) and b == 0):
                        wait_apart(pool, s_scat[q], landed(b - 1, q, ST))
                    for h in range(2):
                        wait_apart(pool, s_eo, b * 2 + h + 1)
                        for a in range(h * HT, h * HT + HT):
                            pool.indirect_dma_start(out=acc[:, :],
                                                    out_offset=bass.IndirectOffsetOnAxis(ap=idxs[:, par, a:a + 1], axis=0),
                                                    in_=eo[:, par, a, :], in_offset=None, compute_op=ALU.add
                                                    ).then_inc(s_scat[par], 16)
                if live(d):
                    wait(pool, s_trps, (d - 1) * 2)
                    wait(pool, s_score, d - 1)
                    wait_apart(pool, s_idx, d + 1)
                    for a in range(ST):
                        pool.indirect_dma_start(out=xg[:, q, a, :], out_offset=None, in_=rows[:, :],
                                                in_offset=bass.IndirectOffsetOnAxis(ap=idx[:, q, a:a + 1], axis=0)
                                                ).then_inc(s_gath[q][a // HT], 16)

            sweep(pool, routed, 4, 6)

            def final(g, p):
                wait(pool, s_flast, g - 1)
                wait(pool, s_fln, g - 1)
                wait_apart(pool, s_fmv, g + 1)
                pool.tensor_scalar(fveps[:, p], fmv[:, p, :, 1], LN_EPS, None, ALU.add).then_inc(s_fveps, 1)
                wait(pool, s_fveps, g + 1)
                pool.tensor_tensor(frstd[:, p], fveps[:, p], neghalf[:, :], ALU.pow).then_inc(s_frstd, 1)

            for g in range(2):
                final(g, g)
            with pool.Fori(1, NG // 2) as j:
                final(j * 2, 0)
                final(j * 2 + 1, 1)

        @block.scalar
        def _(act):
            for row in (0, 32):
                act.dma_start(brow_s[row:row + 1, 0:3 * TPB * D], brow).then_inc(s_wproj, 16)
            act.dma_start(bcol[:, :], bcols).then_inc(s_wproj, 16)
            act.dma_start(wq_s[:, :], wq).then_inc(s_wproj, 16)
            act.wait_ge(s_wproj, 16 * NPROJ)
            act.wait_ge(s_dve0, NDVE0)
            act.wait_ge(s_pool0, NPOOL0)
            for n in range(3):
                for row in (0, 32):
                    act.activation(bpair[row:row + 1, n, :], brow_s[row:row + 1, n * TPB * D:(n + 1) * TPB * D], ACT.Copy).then_inc(s_bhi, 1)
            act.wait_ge(s_qb, 2)

            def attention(i, par):
                b, q = i - 1, 1 - par
                if live(i):
                    wait(act, s_kps, i + 1)
                    wait(act, s_kf, i - 1)
                    act.activation(nk[:, par], psK[:, :].rearrange("p (t d) -> p t d", d=D), ACT.Relu, scale=-1.0).then_inc(s_nk, 1)
                    wait(act, s_nk, i + 1)
                    act.activation(nk[:, par], nk[:, par], ACT.Exp, scale=-1.0).then_inc(s_ek, 1)
                    wait(act, s_vps, i + 1)
                    wait(act, s_kbps, i - 1)
                    act.activation(v1[:, par, :, 0:D], psV[:, :].rearrange("p (t d) -> p t d", d=D), ACT.Copy).then_inc(s_v, 1)
                if live(i):
                    wait(act, s_qps, i + 1)
                    wait(act, s_qf, i - 1)
                    act.activation(nq[:, par], psQ[:, :], ACT.Relu, bias=nqbias[:, :], scale=-1.0).then_inc(s_nq, 1)
                    wait(act, s_nq, i + 1)
                    act.activation(nq[:, par], nq[:, par], ACT.Exp, scale=-1.0).then_inc(s_eq, 1)
                if live(i):
                    wait(act, s_gps, i + 1)
                    wait(act, s_y, i - 1)
                    act.activation(gate[:, par], psG[:, :].rearrange("p (t d) -> p t d", d=D), ACT.Tanh, scale=0.5).then_inc(s_gate, 1)
                if live(b):
                    wait(act, s_ytps, b + 1)
                    wait(act, s_ops, b - 1)
                    act.activation(yT[:, q], psYT, ACT.Copy).then_inc(s_yT, 1)
                if live(i - 2):
                    wait(act, s_x1tps, i - 1)
                    wait(act, s_lgps, i - 3)
                    act.activation(x1Ts[:, par], psOT[:, :], ACT.Copy).then_inc(s_x1Ts, 1)
                    act.activation(X1T[:, bass.ds((i - 2) * SEQ, SEQ)], psOT[:, :], ACT.Copy).then_inc(s_X1T, 1)
                if live(i - 2):
                    wait(act, s_lgps, i - 1)
                    act.activation(LG[:, bass.ds((i - 2) * TPB, TPB), :], kb_lg.rearrange("p (t e) -> p t e", e=E),
                                   ACT.Copy).then_inc(s_lg, 1)

            sweep(act, attention, LAG)
            act.wait_ge(s_wlater, 16 * NLATER)
            act.activation(iota16[:, :], SE[:, :], ACT.Copy).then_inc(s_iota, 1)
            act.wait_ge(s_soft, 2)
            act.activation(LG[:, :, :], LG[:, :, :], ACT.Exp).then_inc(s_exp, 1)

            def shared(i, par):
                b, q = i - 1, 1 - par
                if live(i):
                    for c in range(SC):
                        wait(act, s_sgps, i * SC + c + 1)
                        wait(act, s_hs, (i - 1) * SC + c + 1)
                        act.activation(sgg[:, c], psSG[c][:, :], ACT.Gelu).then_inc(s_sgg, 1)
                        wait(act, s_sups, i * SC + c + 1)
                        act.activation(suc[:, c], psSU[c][:, :], ACT.Copy).then_inc(s_suc, 1)
                if isinstance(i, int) and i == 0:
                    act.wait_ge(s_sT, 1)
                    act.wait_ge(s_iota, 1)
                    act.activation(SE[:, :].rearrange("p (h n) -> p h n", h=2), wide[:, :, :], ACT.Copy).then_inc(s_SE, 1)
                if live(b):
                    wait(act, s_sops, b + 1)
                    if not (isinstance(b, int) and b < 2):
                        act.wait_ge(s_accst[q], landed(b - 2, q))
                    act.activation(so[:, q], psSO[:, :].rearrange("p (t d) -> p t d", d=D), ACT.Copy).then_inc(s_so, 1)

            sweep(act, shared, 1)

            def routed(i, par):
                b, c = i - 3, i - 2

                def high(k):
                    wait(act, s_h, b * 2 * IC + k + 1)
                    wait(act, s_eops, b * 2 - 1 + k // IC)
                    act.activation(hTh[:, k % IC, k // IC * HALF:(k // IC + 1) * HALF], hraw[:, k % 2], ACT.Copy).then_inc(s_hhi, 1)

                for k in range(2 * IC):
                    if live(b):
                        wait(act, s_ggps, b * 2 * IC + k + 1)
                        wait(act, s_h, b * 2 * IC + k - 1)
                        act.activation(gg[:, k % 2], psGG[k % 2][:, :], ACT.Gelu).then_inc(s_gg, 1)
                        if k:
                            high(k - 1)
                    if live(c) and k in WEIGHTS_AT:
                        n = WEIGHTS_AT.index(k)
                        act.wait_ge(s_wt[par], landed(c, par, 2))
                        wait(act, s_eops, (c - 1) * 2)
                        if n < 2:
                            act.activation(wguh[:, par, n, :], wgu_s[:, par, n, :], ACT.Copy).then_inc(s_whi, 1)
                        else:
                            act.activation(wdh[:, par], wd_s[:, par], ACT.Copy).then_inc(s_whi, 1)
                if live(b):
                    high(2 * IC - 1)
                for h in range(2):
                    if live(b):
                        wait(act, s_eops, b * 2 + h + 1)
                        wait(act, s_backps, b * 2 - 1 + h)
                        act.activation(eoT[:, h], psX[h][:, :], ACT.Copy).then_inc(s_eoT, 1)
                    if live(c):
                        wait(act, s_trps, c * 2 + h + 1)
                        wait(act, s_uups, (c - 1) * 2 * IC + (h + 1) * IC)
                        act.activation(xgTh[:, h * HALF:(h + 1) * HALF], psXT[h][:, :], ACT.Copy).then_inc(s_xhi, 1)

            act.wait_ge(s_acc, NB)
            sweep(act, routed, 3, 6)

            def final(g, p):
                wait(act, s_fshift, g + 1)
                for a in range(FT - 1):
                    v = X1[:, bass.ds(g * FT + a, 1), :].rearrange("p o d -> p (o d)")
                    last = act.activation(v, v, ACT.Identity, bias=fshift[:, p, a:a + 1], scale=frstd[:, p, a:a + 1])
                last.then_inc(s_fln, 1)

            with act.Fori(0, NG // 2) as j:
                final(j * 2, 0)
                final(j * 2 + 1, 1)

        @block.vector
        def _(dve):
            dve.memset(bpair[:, :, :].bitcast(F32), 0.0).then_inc(s_dve0, 1)
            dve.memset(onespair[:, :].bitcast(F32), 0.0).then_inc(s_dve0, 1)
            dve.wait_ge(s_dve0, 2)
            for row in (0, 32):
                dve.memset(onespair[row:row + 1, :].bitcast(F32), 1.0).then_inc(s_dve0, 1)
            dve.wait_ge(s_wproj, 16 * NPROJ)
            dve.tensor_scalar(q1bias[:, :], bcol[:, :], 1.0, None, ALU.add).then_inc(s_qb, 1)
            dve.tensor_scalar(nqbias[:, :], bcol[:, :], -1.0, None, ALU.mult).then_inc(s_qb, 1)
            for n in range(3):
                dve.wait_ge(s_bhi, 2 * n + 2)
                low = bpair[32:33, n, :]
                dve.tensor_tensor(low, brow_s[32:33, n * TPB * D:(n + 1) * TPB * D], low.bitcast(F32), ALU.subtract).then_inc(s_blo, 1)
            dve.wait_ge(s_qb, 2)

            def attention(i, par):
                b, q = i - 1, 1 - par
                if live(b):
                    wait(dve, s_ndps, b + 1)
                    dve.tensor_scalar(den[:, q, 0:TPB - 1], psN3[:, :, D:ND], 2e-6, None, ALU.add)
                    dve.tensor_scalar(den[:, q, TPB - 1], kb_nd[:, D:ND], 2e-6, None, ALU.add).then_inc(s_den, 1)
                    wait(dve, s_den, b + 1)
                    dve.reciprocal(rden[:, q], den[:, q]).then_inc(s_rden, 1)
                    wait(dve, s_rden, b + 1)
                    for some, num in ((slice(0, TPB - 1), psN3[:, :, 0:D]), (slice(TPB - 1, TPB), kb_nd[:, 0:D].unsqueeze(1))):
                        zb = rden[:, q, some].unsqueeze(3).broadcast_to([P, some.stop - some.start, HEADS, HD])
                        last = dve.tensor_tensor(y1[:, q, some].rearrange("p t (h c) -> p t h c", c=HD),
                                                 num.rearrange("p t (h c) -> p t h c", c=HD), zb, ALU.mult)
                    last.then_inc(s_y1, 1)
                    wait(dve, s_y1, b + 1)
                    wait(dve, s_gate, b + 1)
                    wait(dve, s_ytps, b - 1)
                    dve.scalar_tensor_tensor(y[:, q], gate[:, q], 1.0, y1[:, q], ALU.add, ALU.mult).then_inc(s_y, 1)
                if live(i - 2):
                    wait(dve, s_rstd, i - 1)
                    for a in range(TPB):
                        last = dve.tensor_scalar(x1[:, par, a, :], x1[:, par, a, :], mv[:, par, a, 0:1],
                                                 rstd[:, par, a:a + 1], ALU.subtract, ALU.mult)
                    last.then_inc(s_ln, 1)
                if live(i):
                    wait(dve, s_ek, i + 1)
                    wait(dve, s_kbps, i - 1)
                    dve.scalar_tensor_tensor(kf[:, par], psK[:, :].rearrange("p (t d) -> p t d", d=D), 1.0, nk[:, par],
                                             ALU.add, ALU.max).then_inc(s_kf, 1)
                    wait(dve, s_eq, i + 1)
                    wait(dve, s_ndps, i - 1)
                    dve.scalar_tensor_tensor(qf[:, par], psQ[:, :], q1bias[:, :], nq[:, par], ALU.add, ALU.max).then_inc(s_qf, 1)
                    if isinstance(i, int) and i == 0:
                        dve.wait_ge(s_wattn, 16 * NATTN)
                    wait(dve, s_kbps, i + 1)
                    wait(dve, s_ndps, i - 1)
                    dve.tensor_tensor(kvks[:, par, 0:D], kb_kv[:, 0:D], headmask, ALU.mult)
                    dve.tensor_scalar(kvks[:, par, D:ND], headsel2, kb_kv[:, D:D + 1], None, ALU.mult).then_inc(s_kvks, 1)
                if live(b):
                    wait(dve, s_ops, b + 1)
                    wait(dve, s_xb, b + 1)
                    if not (isinstance(b, int) and b < 2):
                        dve.wait_ge(s_row[q], landed(b - 2, q))
                    wait(dve, s_X1, b - 1)
                    wait(dve, s_x1tps, b - 1)
                    dve.tensor_tensor(x1[:, q], psOT[:, :].rearrange("p (t d) -> p t d", t=TPB), xb[:, q], ALU.add).then_inc(s_r, 1)
                    wait(dve, s_r, b + 1)
                    wait(dve, s_mv, b)
                    for a in range(TPB):
                        last = dve.bn_stats(bns[:, a, :], x1[:, q, a, :])
                    last.then_inc(s_bns, 1)
                    wait(dve, s_ln, b - 1)
                    wait_apart(dve, s_bns, b + 1)
                    for a in range(TPB):
                        last = dve.bn_aggr(mv[:, q, a, :], bns[:, a, :])
                    last.then_inc(s_mv, 1)

            sweep(dve, attention, LAG)

            dve.wait_ge(s_lg, NB)
            per_e = [P, NT, E]
            dve.tensor_reduce(stat[:, 0], LG[:, :, :], AX.X, ALU.max).then_inc(s_soft, 1)
            dve.wait_ge(s_soft, 1)
            dve.tensor_tensor(LG[:, :, :], LG[:, :, :], stat[:, 0].unsqueeze(2).broadcast_to(per_e), ALU.subtract).then_inc(s_soft, 1)
            dve.tensor_copy(ident16[:, :], ident).then_inc(s_cast, 1)
            dve.tensor_copy(diff16[:, :], cst[:, C_DIFF:C_DIFF + P]).then_inc(s_cast, 1)
            dve.wait_ge(s_exp, 1)
            dve.tensor_reduce(stat[:, 1], LG[:, :, :], AX.X, ALU.add).then_inc(s_soft, 1)
            dve.wait_ge(s_soft, 3)
            dve.reciprocal(stat[:, 2], stat[:, 1]).then_inc(s_soft, 1)
            dve.wait_ge(s_soft, 4)
            for g in range(8):
                tiles = slice(g, NT, 8)
                last = dve.tensor_tensor(S[:, g], LG[:, tiles, :], stat[:, 2, tiles].unsqueeze(2).broadcast_to([P, NT // 8, E]), ALU.mult)
            last.then_inc(s_soft, 1)

            halves = SE[:, :].bitcast(U16).rearrange("p (n h) -> p n h", h=2)
            dve.memset(cand[:, :], float(2 ** (NTOP - 1))).then_inc(s_bit, 1)
            dve.memset(bit[:, 0:1], float(2 ** (NTOP - 1))).then_inc(s_bit, 1)
            dve.memset(quota[:, :], float(CAP)).then_inc(s_quota, 1)
            dve.wait_ge(s_SE, 1)
            dve.tensor_copy(top[:, :], halves[:, :, 1]).then_inc(s_top, 1)
            dve.wait_ge(s_bit, 2)
            dve.wait_ge(s_quota, 1)
            dve.wait_ge(s_top, 1)

            def search(bits, n, k, par):
                q = 1 - par
                wait(dve, s_cand, n - 1)
                dve.tensor_scalar(junk[:, :], bits[:, :], cand[:, :], None, ALU.is_ge, ALU.add, accum_out=cnt[:, :]).then_inc(s_cnt, 1)
                dve.tensor_scalar(bit[:, q:q + 1], bit[:, par:par + 1], 0.5, None, ALU.mult).then_inc(s_bit, 1)
                dve.wait_ge(s_tot, k)
                dve.tensor_scalar(step[:, :], psTOT[:, 0:1], quota[:, :], bit[:, par:par + 1], ALU.is_ge, ALU.mult).then_inc(s_step, 1)
                dve.wait_ge(s_bit, n + 2 * (1 + (bits is rest)))
                dve.wait_ge(s_step, n)
                dve.scalar_tensor_tensor(cand[:, :], step[:, :], bit[:, q:q + 1], cand[:, :], ALU.subtract, ALU.add).then_inc(s_cand, 1)

            for n in (1, 2):
                search(top, n, n, (n - 1) % 2)
            with dve.Fori(1, NTOP // 2) as j:
                search(top, j * 2 + 1, j * 2 + 1, 0)
                search(top, j * 2 + 2, j * 2 + 2, 1)
            dve.wait_ge(s_cand, NTOP)
            dve.tensor_scalar(thrf[:, :], cand[:, :], 0.5, None, ALU.subtract).then_inc(s_thr, 1)
            dve.wait_ge(s_thr, 1)
            dve.tensor_scalar(junk[:, :], top[:, :], thrf[:, :], None, ALU.is_gt, ALU.add, accum_out=cnt[:, :]).then_inc(s_cnt, 1)
            dve.scalar_tensor_tensor(rest[:, :], top[:, :], thrf[:, :], halves[:, :, 0], ALU.is_equal, ALU.mult).then_inc(s_top, 1)
            dve.tensor_scalar(thr_top[:, :], thrf[:, :], float(2 ** 16), None, ALU.mult).then_inc(s_thr, 1)
            dve.memset(cand[:, :], float(2 ** (NREST - 1))).then_inc(s_bit, 1)
            dve.memset(bit[:, 0:1], float(2 ** (NREST - 1))).then_inc(s_bit, 1)
            dve.wait_ge(s_tot, NTOP + 1)
            dve.tensor_scalar(quota[:, :], psTOT[:, 0:1], -1.0, float(CAP), ALU.mult, ALU.add).then_inc(s_quota, 1)
            dve.wait_ge(s_quota, 2)
            dve.wait_ge(s_top, 2)

            dve.wait_ge(s_bit, NTOP + 4)
            with dve.Fori(NTOP // 2, (NTOP + NREST) // 2) as j:
                search(rest, j * 2 + 1, j * 2 + 2, 0)
                search(rest, j * 2 + 2, j * 2 + 3, 1)
            dve.wait_ge(s_cand, NTOP + NREST)
            dve.tensor_scalar(thr_rest[:, :], cand[:, :], 0.5, None, ALU.subtract).then_inc(s_thr, 1)
            dve.wait_ge(s_thr, 3)
            dve.tensor_tensor(thr[:, :], thr_top[:, :], thr_rest[:, :], ALU.bitwise_or).then_inc(s_thr, 1)
            dve.wait_ge(s_thr, 4)
            vth = thr[:, :].bitcast(F32)

            dve.tensor_scalar(gtm[:, :], SE[:, :], vth, None, ALU.is_gt, ALU.add, accum_out=tiecnt[:, 0:1]).then_inc(s_pick, 1)
            dve.tensor_scalar(eqm[:, :], SE[:, :], vth, None, ALU.is_equal, ALU.add, accum_out=tiecnt[:, 1:2]).then_inc(s_pick, 1)
            dve.wait_ge(s_pickps, 1)
            dve.tensor_scalar(need[:, :], psTOT[:, 0:1], -1.0, float(CAP), ALU.mult, ALU.add).then_inc(s_pick, 1)
            dve.tensor_copy(tieoff[:, :], psTOT[:, 1:2]).then_inc(s_pick, 1)
            dve.wait_ge(s_pick, 4)
            dve.tensor_tensor_scan(rank[:, :], eqm[:, :], eqm[:, :], tieoff[:, :], ALU.add, ALU.max).then_inc(s_pick, 1)
            dve.wait_ge(s_pick, 5)
            dve.scalar_tensor_tensor(tiesel[:, :], rank[:, :], need[:, :], eqm[:, :], ALU.is_le, ALU.mult).then_inc(s_pick, 1)
            dve.wait_ge(s_pick, 6)
            dve.tensor_tensor(sel[:, :], tiesel[:, :], gtm[:, :], ALU.add).then_inc(s_pick, 1)
            dve.wait_ge(s_pickps, 2)
            selT = psTOT[:, :].bitcast(F16).rearrange("p (g c e) -> p g c e", g=8, c=8)
            for c in range(8):
                last = dve.tensor_copy(M[:, :, c * 8:c * 8 + 8], selT[:, :, c, :].rearrange("p g e -> p e g"))
            last.then_inc(s_pick, 1)
            dve.wait_ge(s_pick, 8)
            flat = [t[:, :, :].rearrange("p e t -> p (e t)") for t in (M, G)]
            dve.tensor_tensor_scan(flat[1], flat[0], flat[0], 0.0, ALU.add, ALU.max).then_inc(s_pick, 1)
            dve.wait_ge(s_pick, 9)
            dve.tensor_copy(gprev[:, 1:E], G[:, 0:E - 1, NT - 1]).then_inc(s_pick, 1)
            dve.wait_ge(s_pick, 10)
            dve.tensor_tensor(nsel[:, :], G[:, :, NT - 1], gprev[:, :], ALU.subtract).then_inc(s_pick, 1)
            dve.wait_ge(s_pickps, 3)
            dve.tensor_copy(off[:, 0:E], psTOT[:, 0:E]).then_inc(s_pick, 1)
            dve.wait_ge(s_pick, 12)
            dve.tensor_tensor(base[:, :], off[:, 0:E], gprev[:, :], ALU.subtract).then_inc(s_pick, 1)
            dve.wait_ge(s_pick, 13)
            dve.tensor_tensor(C16[:, :, :], G[:, :, :], base[:, :].unsqueeze(2).broadcast_to([P, E, NT]), ALU.add).then_inc(s_pick, 1)
            dve.tensor_copy(tab[:, :, NT], cst[:, C_BLK:C_BLK + E]).then_inc(s_pick, 1)

            def first_slots(e):
                wait_apart(dve, s_cps, e)
                dve.tensor_scalar(U[:, :], iota16[:, :], off[:, bass.ds(e, 1)], None, ALU.is_ge).then_inc(s_U, 1)

            dve.wait_ge(s_iota, 1)
            first_slots(0)
            dve.wait_ge(s_pickps, 4)
            for h in range(2):
                last = dve.tensor_copy(tab[:, h * 8:h * 8 + 8, 0:NT], wide[:, h, :].rearrange("p (e t) -> p e t", t=NT))
            last.then_inc(s_pick, 1)

            def routed(i, par):
                b, c, q = i - 3, i - 2, 1 - par

                def weights_low(n):
                    wait(dve, s_whi, c * 3 + n + 1)
                    if n < 2:
                        dve.tensor_tensor(wgul[:, par, n, :], wgu_s[:, par, n, :], wguh[:, par, n, :].bitcast(F32),
                                          ALU.subtract).then_inc(s_wlo, 1)
                    else:
                        dve.tensor_tensor(wdl[:, par], wd_s[:, par], wdh[:, par].bitcast(F32), ALU.subtract).then_inc(s_wlo, 1)

                def low(k):
                    part = slice(k // IC * HALF, (k // IC + 1) * HALF)
                    wait(dve, s_hhi, b * 2 * IC + k + 1)
                    dve.tensor_tensor(hTl[:, k % IC, part], hraw[:, k % 2], hTh[:, k % IC, part].bitcast(F32),
                                      ALU.subtract).then_inc(s_hlo, 1)

                if live(i):
                    first_slots(i + 1)
                for k in range(2 * IC):
                    if live(b):
                        wait(dve, s_gg, b * 2 * IC + k + 1)
                        wait(dve, s_uups, b * 2 * IC + k + 1)
                        wait(dve, s_hlo, b * 2 * IC + k - 1)
                        dve.tensor_tensor(hraw[:, k % 2], gg[:, k % 2], psUU[k % 2][:, :], ALU.mult).then_inc(s_h, 1)
                        if k:
                            low(k - 1)
                    if live(c) and k == 0:
                        weights_low(0)
                if live(b):
                    low(2 * IC - 1)
                if live(c):
                    if not (isinstance(c, int) and c < 2):
                        dve.wait_ge(s_scat[par], landed(c - 2, par, ST))
                    wait_apart(dve, s_idx, c + 1)
                    dve.tensor_copy(idxs[:, par], idx[:, par]).then_inc(s_idxs, 1)
                if live(i):
                    cs = wide[:, :, 0:HT * (NT + 1)].rearrange("p h (a t) -> p h a t", t=NT + 1)
                    wait(dve, s_cps, i + 1)
                    wait(dve, s_cntt, i)
                    for h in range(2):
                        last = dve.tensor_tensor(cmp[:, h * HT:h * HT + HT, :], cs[:, h, :, 0:NT],
                                                 slotno[:, h * HT:h * HT + HT].unsqueeze(2).broadcast_to([P, HT, NT]), ALU.is_le)
                    last.then_inc(s_cmp, 1)
                    wait(dve, s_cmp, i + 1)
                    wait(dve, s_idx, i)
                    dve.tensor_reduce(cntt[:, :], cmp[:, :, :], AX.X, ALU.add).then_inc(s_cntt, 1)
                    if live(c):
                        wait(dve, s_idxs, c + 1)
                        for h in range(2):
                            dve.wait_ge(s_gath[par][h], landed(c, par, HT))
                    wait(dve, s_cntt, i + 1)
                    dve.scalar_tensor_tensor(idx[:, par].rearrange("p (h a) -> p h a", h=2),
                                             cntt[:, :].rearrange("p (h a) -> p h a", h=2), float(P), cs[:, :, :, NT],
                                             ALU.mult, ALU.add).then_inc(s_idx, 1)
                if live(c):
                    for h in range(2):
                        part = slice(h * HALF, (h + 1) * HALF)
                        wait(dve, s_xhi, c * 2 + h + 1)
                        dve.tensor_tensor(xgTl[:, part], psXT[h][:, :], xgTh[:, part].bitcast(F32), ALU.subtract).then_inc(s_xlo, 1)
                        if h == 0:
                            weights_low(1)
                            weights_low(2)
                if live(b):
                    for h in range(2):
                        wait(dve, s_backps, b * 2 + h + 1)
                        if h == 0 and not (isinstance(b, int) and b < 2):
                            dve.wait_ge(s_scat[q], landed(b - 2, q, ST))
                        w = score[:, q, h * HT:h * HT + HT].unsqueeze(2).broadcast_to([P, HT, D])
                        dve.tensor_tensor(eo[:, q, h * HT:h * HT + HT, :], psX[h][:, :].rearrange("p (a d) -> p a d", d=D), w,
                                          ALU.mult).then_inc(s_eo, 1)
                if live(c):
                    wait(dve, s_eo, (c - 1) * 2)
                    for h in range(2):
                        dve.wait_ge(s_gath[par][h], landed(c, par, HT))
                    wait_apart(dve, s_trps, c * 2 + 2)
                    dve.tensor_copy(score[:, par].unsqueeze(2), xg[:, par, :, bass.ds(c + D, 1)]).then_inc(s_score, 1)

            def shared_product(i, par):
                dve.wait_ge(s_hs, i * SC)
                for c in range(SC):
                    dve.wait_ge(s_suc, i * SC + c + 1)
                    dve.wait_ge(s_sops, i - 1)
                    dve.tensor_tensor(hs[:, par, c], sgg[:, c], suc[:, c], ALU.mult).then_inc(s_hs, 1)

            def shared_sum(b, q):
                dve.wait_ge(s_so, b + 1)
                dve.wait_ge(s_acc, b)
                dve.tensor_tensor(so[:, q], so[:, q], X1[:, b * TPB:(b + 1) * TPB, :], ALU.add).then_inc(s_acc, 1)

            routed(0, 0)
            shared_product(NB - 1, 1)
            shared_sum(NB - 2, 0)
            routed(1, 1)
            shared_sum(NB - 1, 1)
            sweep(dve, routed, 3, 6, first=2)

            def final(g, k):
                p = k % 2
                dve.wait_ge(s_fin[k], 16 * (g // FG + 1) if isinstance(g, int) else (g - k) * 4 + 16)
                wait(dve, s_fmv, g)
                for a in range(FT):
                    last = dve.bn_stats(fbns[:, a, :], X1[:, bass.ds(g * FT + a, 1), :].rearrange("p o d -> p (o d)"))
                last.then_inc(s_fbns, 1)
                wait(dve, s_flast, g - 1)
                wait_apart(dve, s_fbns, g + 1)
                for a in range(FT):
                    last = dve.bn_aggr(fmv[:, p, a, :], fbns[:, a, :])
                last.then_inc(s_fmv, 1)

            def shift(g, k):
                p = k % 2
                wait(dve, s_frstd, g + 1)
                wait(dve, s_fln, g - 1)
                dve.scalar_tensor_tensor(fshift[:, p], fmv[:, p, :, 0], -1.0, frstd[:, p], ALU.mult, ALU.mult).then_inc(s_fshift, 1)
                v = X1[:, bass.ds(g * FT + FT - 1, 1), :].rearrange("p o d -> p (o d)")
                dve.tensor_scalar(v, v, fmv[:, p, FT - 1, 0:1], frstd[:, p, FT - 1:FT], ALU.subtract, ALU.mult).then_inc(s_flast, 1)

            for k in range(FG):
                final(k, k)
                if k:
                    shift(k - 1, k - 1)
            with dve.Fori(1, NG // FG) as j:
                for k in range(FG):
                    final(j * FG + k, k)
                    shift(j * FG + k - 1, (k - 1) % FG)
            shift(NG - 1, FG - 1)

        @block.tensor
        def _(pe):
            pe.wait_ge(s_wproj, 16 * NPROJ)
            pe.wait_ge(s_dve0, NDVE0)
            pe.wait_ge(s_pool0, NPOOL0)

            def project(ps, i, par, n):
                if isinstance(i, int) and i == 0:
                    pe.wait_ge(s_blo, n + 1)
                pe.matmul(ps[:, :], onespair[:, :], bpair[:, n, :], start=True, stop=False)
                for a in range(TPB):
                    last = pe.matmul(ps[:, a * D:(a + 1) * D], xTb[:, par, a * P:(a + 1) * P], wkvg_s[:, n * D:(n + 1) * D],
                                     start=False, stop=(a == TPB - 1))
                return last

            def attention(i, par):
                b, q = i - 1, 1 - par
                if live(i):
                    pe.wait_ge(s_xT[par], landed(i, par))
                    wait(pe, s_kf, i)
                    project(psK, i, par, 0).then_inc(s_kps, 1)
                    wait(pe, s_v, i)
                    project(psV, i, par, 1).then_inc(s_vps, 1)
                    wait(pe, s_qf, i)
                    pe.matmul(psQ[:, :], wq_s[:, :], xTb[:, par], start=True, stop=True).then_inc(s_qps, 1)
                    wait(pe, s_gate, i)
                    project(psG, i, par, 2).then_inc(s_gps, 1)
                if isinstance(i, int) and i == 1:
                    pe.wait_ge(s_wattn, 16 * NATTN)
                if live(b):
                    wait(pe, s_y, b + 1)
                    wait(pe, s_yT, b)
                    for a in range(TPB):
                        last = pe.transpose(psYT[:, a * P:(a + 1) * P], y[:, q, a, :], ident)
                    last.then_inc(s_ytps, 1)
                if live(i - 2):
                    wait(pe, s_ln, i - 1)
                    wait(pe, s_r, i - 1)
                    for a in range(TPB):
                        last = pe.transpose(psOT[:, a * P:(a + 1) * P], x1[:, par, a, :], ident)
                    last.then_inc(s_x1tps, 1)
                if live(i):
                    wait(pe, s_kf, i + 1)
                    wait(pe, s_v, i + 1)
                    wait(pe, s_y1, i)
                    wait(pe, s_lg, i - 2)
                    for a in range(TPB):
                        last = pe.matmul(kb_kv, kf[:, par, a, :], v1[:, par, a, :], start=(a == 0), stop=(a == TPB - 1))
                    last.then_inc(s_kbps, 1)
                if live(b):
                    wait(pe, s_yT, b + 1)
                    wait(pe, s_X1T, b)
                    for a in range(TPB):
                        last = pe.matmul(psOT[:, a * D:(a + 1) * D], yT[:, q, a * P:(a + 1) * P], wo_s[:, :], start=True, stop=True)
                    last.then_inc(s_ops, 1)
                if live(i - 2):
                    wait(pe, s_x1Ts, i - 1)
                    wait(pe, s_kvks, min(i + 1, NB) if isinstance(i, int) else i + 1)
                    for a in range(TPB):
                        last = pe.matmul(kb_lg[:, a * E:(a + 1) * E], x1Ts[:, par, a * P:(a + 1) * P], gateT_s[:, :], start=True, stop=True)
                    last.then_inc(s_lgps, 1)
                if live(i):
                    wait(pe, s_kvks, i + 1)
                    wait(pe, s_qf, i + 1)
                    for a in range(TPB):
                        nd = psN3[:, a, :] if a < TPB - 1 else kb_nd
                        if a == TPB - 1:
                            wait(pe, s_lg, i - 1)
                        last = pe.matmul(nd, qf[:, par, a * P:(a + 1) * P], kvks[:, par], start=True, stop=True)
                    last.then_inc(s_ndps, 1)

            sweep(pe, attention, LAG)
            for s in (s_kf, s_v, s_gate, s_qf, s_yT, s_y1, s_r, s_x1Ts, s_X1T, s_lg):
                pe.wait_ge(s, NB)

            def count(n):
                wait(pe, s_cnt, n)
                pe.matmul(psTOT[:, 0:1], same_expert, cnt[:, :], start=True, stop=True).then_inc(s_tot, 1)

            pe.wait_ge(s_wlater, 16 * NLATER)

            COUNTS = 3

            def shared(i, par, counts=COUNTS, middle=None):
                b, q = i - 1, 1 - par

                def between(n):
                    if n <= counts:
                        count((i - 1) * COUNTS + n)

                if live(i):
                    for c in range(SC):
                        wait(pe, s_sgg, i * SC + c - 1)
                        pe.matmul(psSG[c][:, :], wsgu_s[:, 0, c * P:(c + 1) * P], X1T[:, bass.ds(i * SEQ, SEQ)],
                                  start=True, stop=True).then_inc(s_sgps, 1)
                        wait(pe, s_suc, i * SC + c - 1)
                        pe.matmul(psSU[c][:, :], wsgu_s[:, 1, c * P:(c + 1) * P], X1T[:, bass.ds(i * SEQ, SEQ)],
                                  start=True, stop=True).then_inc(s_sups, 1)
                        if isinstance(i, int) and i == 0 and c == 1:
                            pe.wait_ge(s_soft, 5)
                            for g in range(8):
                                last = pe.transpose(wide[:, g // 4, g % 4 * P:(g % 4 + 1) * P], S[:, g].rearrange("p c e -> p (c e)"), ident)
                            last.then_inc(s_sT, 1)
                        between(c + 1)
                if middle:
                    middle()
                if live(b):
                    wait(pe, s_hs, b * SC + SC)
                    wait(pe, s_so, b)
                    for a in range(TPB):
                        for c in range(SC):
                            last = pe.matmul(psSO[:, a * D:(a + 1) * D], hs[:, q, c, a * P:(a + 1) * P], wsd_s[:, c, :],
                                             start=(c == 0), stop=(c == SC - 1))
                    last.then_inc(s_sops, 1)
                    between(3)

            def tie_sums():
                pe.wait_ge(s_pick, 2)
                pe.matmul(psTOT[:, 0:1], same_expert, tiecnt[:, 0:1], start=True, stop=True)
                pe.matmul(psTOT[:, 1:2], earlier_run, tiecnt[:, 1:2], start=True, stop=True).then_inc(s_pickps, 1)

            def turn_selection():
                pe.wait_ge(s_pick, 7)
                pe.wait_ge(s_cast, 2)
                for g in range(8):
                    last = pe.transpose(psTOT[:, :].bitcast(F16)[:, g * P:(g + 1) * P], sel[:, g * P:(g + 1) * P], ident16[:, :])
                last.then_inc(s_pickps, 1)

            def earlier_partitions():
                pe.wait_ge(s_pick, 11)
                pe.matmul(psTOT[:, 0:E], upper, nsel[:, :], start=True, stop=True).then_inc(s_pickps, 1)

            def differences():
                pe.wait_ge(s_pick, 15)
                pe.wait_ge(s_SE, 1)
                for h in range(2):
                    last = pe.matmul(wide[:, h, :], diff16[:, :], C16[:, h * 8:h * 8 + 8, :].rearrange("p e t -> p (e t)"), start=True, stop=True)
                last.then_inc(s_pickps, 1)

            def slots(i):
                wait(pe, s_U, i + 1)
                wait(pe, s_idx, i)
                for a in range(ST):
                    last = pe.matmul(wide[:, a // HT, a % HT * (NT + 1):(a % HT + 1) * (NT + 1)], U[:, a * P:(a + 1) * P],
                                     tab[:, bass.ds(i, 1), :].rearrange("p o t -> p (o t)"), start=True, stop=True)
                last.then_inc(s_cps, 1)

            shared(0, 0, 0)
            shared(1, 1)
            with pe.Fori(1, 5) as j:
                shared(j * 2, 0)
                shared(j * 2 + 1, 1)
            shared(10, 0)
            shared(11, 1, NCOUNT - 10 * COUNTS)
            tie_sums()
            shared(12, 0, 0)
            turn_selection()
            shared(13, 1, 0)
            earlier_partitions()
            shared(14, 0, 0, middle=differences)
            pe.wait_ge(s_pick, 16)
            slots(0)
            shared(15, 1, 0, middle=lambda: slots(1))
            shared(16, 0, 0)
            for s, n in ((s_sgg, SC), (s_suc, SC), (s_so, 1)):
                pe.wait_ge(s, NB * n)
            pe.wait_ge(s_pick, 16)

            def product(ps, lhs, rhs, first, last):
                pe.matmul(ps, lhs[0], rhs[0], start=first, stop=False)
                pe.matmul(ps, lhs[0], rhs[1], start=False, stop=False)
                return pe.matmul(ps, lhs[1], rhs[0], start=False, stop=last)

            def routed(i, par):
                b, c, q = i - 3, i - 2, 1 - par
                if live(i) and not (isinstance(i, int) and i < 2):
                    slots(i)
                if live(b):
                    wait(pe, s_wlo, b * 3 + 3)
                    for h in range(2):
                        part = slice(h * HALF, (h + 1) * HALF)
                        if h == 0:
                            wait(pe, s_xlo, b * 2 + 1)
                        for m in range(IC):
                            k = h * IC + m
                            if k == 1:
                                wait(pe, s_xlo, b * 2 + 2)
                            chunk = slice(m * P, (m + 1) * P)
                            wait(pe, s_gg, b * 2 * IC + k - 1)
                            wait(pe, s_h, b * 2 * IC + k - 1)
                            x2 = (xgTh[:, part], xgTl[:, part])
                            product(psGG[k % 2][:, :], (wguh[:, q, 0, chunk], wgul[:, q, 0, chunk]), x2, True, True).then_inc(s_ggps, 1)
                            product(psUU[k % 2][:, :], (wguh[:, q, 1, chunk], wgul[:, q, 1, chunk]), x2, True, True).then_inc(s_uups, 1)
                for h in range(2):
                    if live(b):
                        wait(pe, s_hlo, b * 2 * IC + (h + 1) * IC)
                        wait(pe, s_eo, b * 2 - 1 + h)
                        part = slice(h * HALF, (h + 1) * HALF)
                        for m in range(IC):
                            last = product(psX[h][:, :], (wdh[:, q, m, :], wdl[:, q, m, :]), (hTh[:, m, part], hTl[:, m, part]),
                                           m == 0, m == IC - 1)
                        last.then_inc(s_eops, 1)
                    if live(c):
                        pe.wait_ge(s_gath[par][h], landed(c, par, HT))
                        wait(pe, s_gg, (c - 1) * 2 * IC + 2 * IC - 1 + h)
                        for a in range(HT):
                            last = pe.transpose(psXT[h][:, a * P:(a + 1) * P], xg[:, par, h * HT + a, 0:D], ident)
                        last.then_inc(s_trps, 1)
                if live(b):
                    for h in range(2):
                        wait(pe, s_eoT, b * 2 + h + 1)
                        for a in range(HT):
                            last = pe.transpose(psX[h][:, a * P:(a + 1) * P], eoT[:, h, a * P:(a + 1) * P], ident)
                        last.then_inc(s_backps, 1)

            sweep(pe, routed, 3, 6)


def kernel(**inputs):
    import concourse.bacc as bacc
    from concourse.bass_utils import run_bass_kernel_spmd

    g = {k: np.ascontiguousarray(v) for k, v in inputs.items()}
    arrays = {
        "x": g["L0_attn_x"],
        "xT": g["L0_attn_x"].transpose(0, 2, 1),
        "wq": g["L0_attn_wq_w"],
        "wkvg": np.concatenate([g["L0_attn_wk_w"], g["L0_attn_wv_w"], g["L0_attn_wg_w"]], axis=1),
        "wo": g["L0_attn_out_w"],
        "bcols": g["L0_attn_wq_b"][:, None],
        "brow": np.tile(np.stack([g["L0_attn_wk_b"], g["L0_attn_wv_b"], g["L0_attn_wg_b"]]), (1, TPB)).reshape(1, -1),
        "bo": np.broadcast_to(g["L0_attn_out_b"][None, :], (P, D)),
        "consts": constants(),
        "iota": np.broadcast_to(np.arange(CAP, dtype=np.float32)[None, :], (P, CAP)),
        "gateT": g["L0_ffn_gate_w"].T,
        "wsgu": np.stack([g["L0_ffn_Sg"].T, g["L0_ffn_Su"].T], axis=1),
        "wsd": g["L0_ffn_Sd"].T.reshape(SC, P, D).transpose(1, 0, 2),
        "wgu": np.stack([g["L0_ffn_Wg"].transpose(0, 2, 1), g["L0_ffn_Wu"].transpose(0, 2, 1)], axis=2),
        "wd": g["L0_ffn_Wd"].transpose(0, 2, 1).reshape(E, IC, P, D).transpose(0, 2, 1, 3),
    }
    arrays = {f"in_{n}": np.ascontiguousarray(a) for n, a in arrays.items()}
    nc = bacc.Bacc("TRN2", target_bir_lowering=False, num_devices=1)
    args = [nc.dram_tensor(n, a.shape, mybir.dt.from_np(a.dtype), kind="ExternalInput").ap() for n, a in arrays.items()]
    args.append(nc.dram_tensor("out", (NB, SEQ, D), F32, kind="ExternalOutput").ap())
    program(nc, *args)
    r = run_bass_kernel_spmd(nc, [arrays], core_ids=[0])
    return r.results[0]["out"]
```

```python
from contextlib import ExitStack

import numpy as np

import concourse.bass as bass
from concourse import mybir

F32 = mybir.dt.float32
F32R = mybir.dt.float32r
F16 = mybir.dt.float16
U16 = mybir.dt.uint16
I32 = mybir.dt.int32
ACT = mybir.ActivationFunctionType
ALU = mybir.AluOpType
AX = mybir.AxisListType

P = 128
D = 128
HEADS = 16
HD = D // HEADS
NB = 16
SEQ = 512
TPB = SEQ // P
T = NB * SEQ
NT = T // P
E = 16
CAP = 2 * T // E
ST = CAP // P
HALF = CAP // 2
HT = ST // 2
I = 512
IC = I // P
SC = 2
ROW = D + E
NC = NT // 8
LN_EPS = 1e-5
WEIGHTS_AT = (0, 4, 6)
LAG = 2
FT = 8
NG = NT // FT
FG = 4

C_IDENT, C_HEAD, C_SAME, C_PREF, C_UPPER, C_DIFF, C_SEL2, C_SLOT, C_BLK, C_END = np.cumsum(
    [0, P, P, P, P, P, P, HEADS, ST, E]).tolist()


def constants():
    c = np.zeros((P, C_END), np.float32)
    r, q = np.arange(P)[:, None], np.arange(P)[None, :]
    c[:, C_IDENT:C_IDENT + P] = r == q
    c[:, C_HEAD:C_HEAD + P] = r // HD == q // HD
    c[:, C_SAME:C_SAME + P] = r % E == q % E
    c[:, C_PREF:C_PREF + P] = (r % E == q % E) & (r // E < q // E)
    c[:, C_UPPER:C_UPPER + P] = r < q
    c[:, C_DIFF:C_DIFF + P] = (r == q) * 1.0 - (r == q - 1) * 1.0
    c[:, C_SEL2:C_SEL2 + HEADS] = 2.0 * (r // HD == np.arange(HEADS)[None, :])
    c[:, C_SLOT:C_SLOT + ST] = r + P * np.arange(ST)[None, :]
    c[:, C_BLK:C_BLK + E] = r >= 1
    return c


def program(nc, x, xT, wq, wkvg, wo, bcols, brow, bv, bo, consts, iota, gateT, wsgu, wsd, wgu, wd, out):
    with ExitStack() as ctx:
        def sb(name, shape, dt=F32):
            return ctx.enter_context(nc.sbuf_tensor(name, shape, dt))

        def region(name, size):
            whole = sb(name, [P, size])

            def layout():
                at = [0]

                def carve(shape, dt=F32):
                    n = int(np.prod(shape[1:]))
                    assert at[0] + n <= size
                    part = whole[:, at[0]:at[0] + n]
                    at[0] += n
                    if dt != F32:
                        part = part.bitcast(dt)
                    dims = "abcd"[:len(shape) - 1]
                    sizes = dict(zip(dims, shape[1:]))
                    return part.rearrange(f"p ({' '.join(dims)}) -> p {' '.join(dims)}", **sizes)

                return carve

            return layout

        def sem(name):
            return ctx.enter_context(nc.semaphore(name))

        def wait(eng, s, v):
            if not (isinstance(v, int) and v <= 0):
                eng.wait_ge(s, v)

        def wait_apart(eng, s, v):
            wait(eng, s, v)
            if not isinstance(v, int):
                eng.sem_inc(s_apart, 1)

        def landed(i, par, ndma=1):
            return 16 * ndma * (i // 2 + 1) if isinstance(i, int) else (i - par) * (8 * ndma) + 16 * ndma

        def live(b, n=NB):
            return not isinstance(b, int) or 0 <= b < n

        def sweep(eng, step, lag, peel=4, first=0, stop=NB):
            for i in range(first, peel):
                step(i, i % 2)
            with eng.Fori(peel // 2, stop // 2) as j:
                step(j * 2, 0)
                step(j * 2 + 1, 1)
            for i in range(stop, stop + lag):
                step(i, i % 2)

        rows = nc.dram_tensor("rows", [T, ROW], F32, kind="Internal").ap()
        acc = nc.dram_tensor("acc", [T, D], F32, kind="Internal").ap()
        rows_tok = rows.rearrange("(t p) r -> p t r", p=P)
        acc_tok = acc.rearrange("(t p) d -> p t d", p=P)
        x_tok = x.rearrange("b (t p) d -> p (b t) d", p=P)
        out_tok = out.rearrange("b (t p) d -> p (b t) d", p=P)

        cst = sb("cst", [P, C_END])
        ident = cst[:, C_IDENT:C_IDENT + P]
        headmask = cst[:, C_HEAD:C_HEAD + P]
        same_expert = cst[:, C_SAME:C_SAME + P]
        earlier_run = cst[:, C_PREF:C_PREF + P]
        upper = cst[:, C_UPPER:C_UPPER + P]
        headsel2 = cst[:, C_SEL2:C_SEL2 + HEADS]
        slotno = cst[:, C_SLOT:C_SLOT + ST]
        ident16 = sb("ident16", [P, P], F16)
        diff16 = sb("diff16", [P, P], F16)
        iota16 = sb("iota16", [P, CAP], F16)
        wq_s, wo_s = sb("wq_s", [P, D]), sb("wo_s", [P, D])
        wkvg_s = sb("wkvg_s", [P, 3 * D])
        bcol = sb("bcol", [P, 1])
        q1bias, nqbias = sb("q1bias", [P, 1]), sb("nqbias", [P, 1])
        bpair = sb("bpair", [33, 2, TPB * D], F32R)
        onespair = sb("onespair", [33, P], F32R)
        bv_s = sb("bv_s", [P, D])
        bo_s = sb("bo_s", [P, TPB, D])
        neghalf = sb("neghalf", [P, FT])
        gateT_s = sb("gateT_s", [P, E])
        wsgu_s = sb("wsgu_s", [P, 2, SC * P])
        wsd_s = sb("wsd_s", [P, SC, D])

        work = region("work", 16640)
        at = work()
        xTb = at([P, 2, SEQ])
        xt, xb, x1 = (at([P, 2, TPB, D]) for _ in range(3))
        x1Ts = at([P, 2, SEQ])
        nk, kf, gate = (at([P, 2, TPB, D]) for _ in range(3))
        v1 = at([P, 2, TPB, D + 1])
        nq, qf = at([P, 2, SEQ]), at([P, 2, SEQ])
        kvh = at([P, D])
        kvks = at([P, 2, D + HEADS])
        den, rden = at([P, 2, TPB, HEADS]), at([P, 2, TPB, HEADS])
        y1, y = at([P, 2, TPB, D]), at([P, 2, TPB, D])
        yT = at([P, 2, SEQ])
        bns = at([P, TPB, 6])
        mv = at([P, 2, TPB, 2])
        veps, rstd = at([P, 2, TPB]), at([P, 2, TPB])

        LG = sb("LG", [P, NT, E])
        S = sb("S", [P, 8, NT // 8, E])
        SE = sb("SE", [P, CAP])
        stat = sb("stat", [P, 3, NT])
        top = sb("top", [P, CAP], U16)
        rest = sb("rest", [P, CAP], U16)
        junk = sb("junk", [P, CAP], F16)
        cnt, ge = sb("cnt", [P, 3]), sb("ge", [P, 3])
        cand, cand_next, times = (sb(n, [P, 4]) for n in ("cand", "cand_next", "times"))
        unit = sb("unit", [P, 2, 4])
        step, quota, thrf = (sb(n, [P, 1]) for n in ("step", "quota", "thrf"))
        thr_top, thr_rest, thr = (sb(n, [P, 1], I32) for n in ("thr_top", "thr_rest", "thr"))
        tiecnt = sb("tiecnt", [P, 2])
        need, tieoff = sb("need", [P, 1]), sb("tieoff", [P, 1])
        gtm, eqm, tiesel, sel = (sb(n, [P, CAP], F16) for n in ("gtm", "eqm", "tiesel", "sel"))
        rank = sb("rank", [P, CAP])
        M = sb("M", [P, E, NT])
        G = sb("G", [P, E, NT])
        gprev, nsel, base = (sb(n, [P, E]) for n in ("gprev", "nsel", "base"))
        off = sb("off", [P, E + 1])
        C16 = sb("C16", [P, E, NT], F16)
        tab = sb("tab", [P, E, NT + 1], F16)
        U = sb("U", [P, CAP], F16)

        cmp = sb("cmp", [P, ST, NT])
        cntt = sb("cntt", [P, ST])
        idx = sb("idx", [P, 2, ST], I32)
        idxs = sb("idxs", [P, 2, ST], I32)
        at = work()
        xg = at([P, 2, ST, ROW])
        wgu_s = at([P, 2, 2, I])
        wd_s = at([P, 2, IC, D])
        sgg, suc = at([P, SC, SEQ]), at([P, SC, SEQ])
        hs = at([P, 2, SC, SEQ])
        so = at([P, 2, TPB, D])
        gg, hraw = at([P, 2, HALF]), at([P, 2, HALF])
        eoT = at([P, 2, HALF])
        score = at([P, 2, ST])
        eo = at([P, 2, ST, D])
        at = work()
        fbns, fmv = at([P, FT, 6]), at([P, 2, FT, 2])
        fveps, frstd, fshift = (at([P, 2, FT]) for _ in range(3))

        with nc.sbuf_tensor("X1", [P, NT, D], F32) as X1, nc.sbuf_tensor("X1T", [P, T], F32) as X1T:
            pass
        brow_s = X1T
        hTh, hTl = sb("hTh", [P, IC, CAP], F32R), sb("hTl", [P, IC, CAP], F32R)
        wguh, wgul = sb("wguh", [P, 2, 2, I], F32R), sb("wgul", [P, 2, 2, I], F32R)
        wdh, wdl = sb("wdh", [P, 2, IC, D], F32R), sb("wdl", [P, 2, IC, D], F32R)
        xgTh, xgTl = sb("xgTh", [P, CAP], F32R), sb("xgTl", [P, CAP], F32R)

        bank = [ctx.enter_context(nc.psum_tensor(f"bank{n}", [P, 512], F32)) for n in range(6)]
        wide = ctx.enter_context(nc.psum_tensor("wide", [P, 2, 512], F32))
        psK, psV, psG, psQ, psN, psOT = bank
        psYT, psKB = wide[:, 0, :], wide[:, 1, :]
        ND = D + HEADS
        kb_kv, kb_nd, kb_lg = psKB[:, 0:D + 1], psKB[:, ND:2 * ND], psKB[:, 2 * ND:2 * ND + TPB * E]
        psN3 = psN[:, 0:(TPB - 1) * ND].rearrange("p (t n) -> p t n", n=ND)
        psSG, psSU, psSO, psTOT = bank[0:2], bank[2:4], bank[4], bank[5]
        psX, psGG, psUU = bank[0:2], bank[2:4], bank[4:6]
        psXT = psGG

        s_apart, s_pool0, s_dve0, s_bhi, s_blo, s_qb = (sem(n) for n in ("s_apart", "s_pool0", "s_dve0", "s_bhi", "s_blo", "s_qb"))
        s_wbias, s_wproj, s_wattn, s_wlater, s_iota, s_cast = (sem(n) for n in ("s_wbias", "s_wproj", "s_wattn", "s_wlater", "s_iota", "s_cast"))
        s_xT = [sem(f"s_xT{n}") for n in range(2)]
        s_xt = [sem(f"s_xt{n}") for n in range(2)]
        s_kps, s_vps, s_qps, s_gps = (sem(n) for n in ("s_kps", "s_vps", "s_qps", "s_gps"))
        s_nk, s_ek, s_v, s_nq, s_eq, s_gate = (sem(n) for n in ("s_nk", "s_ek", "s_v", "s_nq", "s_eq", "s_gate"))
        s_kf, s_qf, s_xb = sem("s_kf"), sem("s_qf"), sem("s_xb")
        s_kbps, s_kvh, s_bv, s_kvks, s_ndps = (sem(n) for n in ("s_kbps", "s_kvh", "s_bv", "s_kvks", "s_ndps"))
        s_den, s_rden, s_y1, s_y, s_ytps, s_yT = (sem(n) for n in ("s_den", "s_rden", "s_y1", "s_y", "s_ytps", "s_yT"))
        s_ops, s_r, s_bns, s_mv, s_veps, s_rstd, s_ln = (
            sem(n) for n in ("s_ops", "s_r", "s_bns", "s_mv", "s_veps", "s_rstd", "s_ln"))
        s_x1tps, s_x1Ts, s_lgps, s_lg, s_X1, s_X1T = (
            sem(n) for n in ("s_x1tps", "s_x1Ts", "s_lgps", "s_lg", "s_X1", "s_X1T"))
        s_row = [sem(f"s_row{n}") for n in range(2)]
        s_soft, s_exp, s_score_rows = sem("s_soft"), sem("s_exp"), sem("s_score_rows")
        s_sgps, s_sups, s_sops = sem("s_sgps"), sem("s_sups"), sem("s_sops")
        s_sgg, s_suc, s_hs, s_so, s_acc = (sem(n) for n in ("s_sgg", "s_suc", "s_hs", "s_so", "s_acc"))
        s_accst = [sem(f"s_accst{n}") for n in range(2)]
        s_sT, s_SE, s_cnt, s_tot, s_step, s_thr, s_cand, s_bit, s_top, s_quota, s_next = (
            sem(n) for n in ("s_sT", "s_SE", "s_cnt", "s_tot", "s_step", "s_thr", "s_cand", "s_bit", "s_top", "s_quota", "s_next"))
        s_pick, s_pickps = sem("s_pick"), sem("s_pickps")
        s_U, s_cps, s_cmp, s_cntt, s_idx = (sem(n) for n in ("s_U", "s_cps", "s_cmp", "s_cntt", "s_idx"))
        s_wt = [sem(f"s_wt{n}") for n in range(2)]
        s_gath = [[sem(f"s_gath{n}{h}") for h in range(2)] for n in range(2)]
        s_scat = [sem(f"s_scat{n}") for n in range(2)]
        s_trps, s_xhi, s_xlo, s_whi, s_wlo, s_idxs, s_score, s_eoT, s_backps = (
            sem(n) for n in ("s_trps", "s_xhi", "s_xlo", "s_whi", "s_wlo", "s_idxs", "s_score", "s_eoT", "s_backps"))
        s_ggps, s_uups, s_gg, s_h, s_hhi, s_hlo, s_eops, s_eo = (
            sem(n) for n in ("s_ggps", "s_uups", "s_gg", "s_h", "s_hhi", "s_hlo", "s_eops", "s_eo"))
        s_fin = [sem(f"s_fin{n}") for n in range(FG)]
        s_fbns, s_fmv, s_fveps, s_frstd, s_fshift, s_flast, s_fln, s_out = (
            sem(n) for n in ("s_fbns", "s_fmv", "s_fveps", "s_frstd", "s_fshift", "s_flast", "s_fln", "s_out"))
        NPROJ, NATTN, NLATER = 3, 5, 3
        NPOOL0, NDVE0 = 9, 4
        NTOP, NREST = 7, 8
        SOFT = 5
        SPLIT = NC - 1
        NCOUNT = NTOP + 1 + NREST

        block = ctx.enter_context(nc.Block())

        @block.sync
        def _(sp):
            def attention(i, par):
                if live(i):
                    wait(sp, s_gps, i - 1)
                    sp.dma_start(xTb[:, par, :], xT[bass.ds(i, 1)].rearrange("o p n -> p (o n)")).then_inc(s_xT[par], 16)
                    wait(sp, s_xb, i - 1)
                    sp.dma_start(xt[:, par], x_tok[:, bass.ds(i * TPB, TPB), :]).then_inc(s_xt[par], 16)
                if isinstance(i, int) and i == 0:
                    for dst, src in ((cst[:, :], consts), (bv_s[:, :], bv), (bo_s[:, :, :], bo.unsqueeze(1).broadcast_to([P, TPB, D])),
                                     (wo_s[:, :], wo), (gateT_s[:, :], gateT)):
                        sp.dma_start(dst, src).then_inc(s_wattn, 16)
                    for dst, src in ((SE[:, :], iota), (wsgu_s[:, :, :], wsgu), (wsd_s[:, :, :], wsd)):
                        sp.dma_start(dst, src).then_inc(s_wlater, 16)
                if live(i - 2):
                    wait(sp, s_ln, i - 1)
                    sp.dma_start(rows_tok[:, bass.ds((i - 2) * TPB, TPB), 0:D], x1[:, par]).then_inc(s_row[par], 16)

            sp.dma_start(wkvg_s[:, :], wkvg).then_inc(s_wproj, 16)
            sweep(sp, attention, LAG)
            def weights(e, par):
                wait(sp, s_wlo, (e - 1) * 3)
                sp.dma_start(wgu_s[:, par], wgu[bass.ds(e, 1)].rearrange("o p g i -> p (o g) i")).then_inc(s_wt[par], 16)
                sp.dma_start(wd_s[:, par], wd[bass.ds(e, 1)].rearrange("o p c d -> p (o c) d")).then_inc(s_wt[par], 16)

            for par in range(2):
                sp.wait_ge(s_row[par], 16 * (NB // 2))
            for s in (s_X1, s_X1T, s_lgps, s_y, s_yT):
                sp.wait_ge(s, NB)
            for e in range(2):
                weights(e, e)
            sp.wait_ge(s_soft, 2 * SOFT)
            for g in range(8):
                sp.dma_start(rows_tok.rearrange("p (c g) r -> p g c r", g=8)[:, g, :, D:ROW], S[:, g]).then_inc(s_score_rows, 16)

            def shared(i, par):
                b, q = i - 1, 1 - par
                if live(b):
                    wait(sp, s_acc, b + 1)
                    sp.dma_start(acc_tok[:, bass.ds(b * TPB, TPB), :], so[:, q]).then_inc(s_accst[q], 16)

            sweep(sp, shared, 1)

            sweep(sp, weights, 0, first=2)
            for par in range(2):
                sp.wait_ge(s_scat[par], 16 * ST * (E // 2))

            def load(g, k):
                wait(sp, s_fbns, g - FG + 1)
                sp.dma_start(X1[:, bass.ds(g * FT, FT), :], acc_tok[:, bass.ds(g * FT, FT), :]).then_inc(s_fin[k], 16)

            for k in range(FG):
                load(k, k)
            with sp.Fori(1, NG // FG) as j:
                for k in range(FG):
                    load(j * FG + k, k)
            with sp.Fori(0, NG) as g:
                sp.wait_ge(s_fln, g + 1)
                sp.wait_ge(s_flast, g + 1)
                sp.dma_start(out_tok[:, bass.ds(g * FT, FT), :], X1[:, bass.ds(g * FT, FT), :]).then_inc(s_out, 16)
            sp.wait_ge(s_out, 16 * NG)

        @block.gpsimd
        def _(pool):
            pool.memset(v1[:, 0, :, D:D + 1], 1.0).then_inc(s_pool0, 1)
            pool.memset(v1[:, 1, :, D:D + 1], 1.0).then_inc(s_pool0, 1)
            pool.memset(neghalf[:, :], -0.5).then_inc(s_pool0, 1)
            pool.memset(gprev[:, :], 0.0).then_inc(s_pool0, 1)
            pool.memset(off[:, E:E + 1], 0.0).then_inc(s_pool0, 1)
            for n in range(4):
                pool.memset(times[:, n:n + 1], float(n)).then_inc(s_pool0, 1)
            pool.wait_ge(s_pool0, NPOOL0)
            pool.wait_ge(s_wattn, 16 * NATTN)

            def attention(i, par):
                b, q = i - 1, 1 - par
                if live(i):
                    pool.wait_ge(s_xt[par], landed(i, par))
                    wait(pool, s_r, i - 1)
                    pool.tensor_tensor(xb[:, par], xt[:, par], bo_s[:, :, :], ALU.add).then_inc(s_xb, 1)
                if live(i - 2):
                    wait(pool, s_ln, i - 1)
                    pool.tensor_copy(X1[:, bass.ds((i - 2) * TPB, TPB), :], x1[:, par]).then_inc(s_X1, 1)
                if live(b):
                    wait_apart(pool, s_mv, b + 1)
                    pool.tensor_scalar(veps[:, q], mv[:, q, :, 1], LN_EPS, None, ALU.add).then_inc(s_veps, 1)
                    wait(pool, s_veps, b + 1)
                    pool.tensor_tensor(rstd[:, q], veps[:, q], neghalf[:, 0:TPB], ALU.pow).then_inc(s_rstd, 1)

            sweep(pool, attention, LAG)

            def shared(i, par):
                b, q = i - 1, 1 - par
                if live(i):
                    for c in range(SC):
                        wait(pool, s_suc, i * SC + c + 1)
                        wait(pool, s_sops, i - 1)
                        pool.tensor_tensor(hs[:, par, c], sgg[:, c], suc[:, c], ALU.mult).then_inc(s_hs, 1)
                if live(b):
                    wait(pool, s_so, b + 1)
                    pool.tensor_tensor(so[:, q], so[:, q], X1[:, bass.ds(b * TPB, TPB), :], ALU.add).then_inc(s_acc, 1)

            sweep(pool, shared, 1, stop=NB - 2)
            for par in range(2):
                pool.wait_ge(s_row[par], 16 * (NB // 2))
            pool.wait_ge(s_score_rows, 16 * 8)

            def routed(i, par):
                b, d, q = i - 4, i - 1, 1 - par
                if live(b):
                    if isinstance(b, int) and b == 0:
                        for n in range(2):
                            pool.wait_ge(s_accst[n], 16 * (NB // 2))
                    if not (isinstance(b, int) and b == 0):
                        wait_apart(pool, s_scat[q], landed(b - 1, q, ST))
                    for h in range(2):
                        wait_apart(pool, s_eo, b * 2 + h + 1)
                        for a in range(h * HT, h * HT + HT):
                            pool.indirect_dma_start(out=acc[:, :],
                                                    out_offset=bass.IndirectOffsetOnAxis(ap=idxs[:, par, a:a + 1], axis=0),
                                                    in_=eo[:, par, a, :], in_offset=None, compute_op=ALU.add
                                                    ).then_inc(s_scat[par], 16)
                if live(d):
                    wait(pool, s_trps, (d - 1) * 2)
                    wait(pool, s_score, d - 1)
                    wait_apart(pool, s_idx, d + 1)
                    for a in range(ST):
                        pool.indirect_dma_start(out=xg[:, q, a, :], out_offset=None, in_=rows[:, :],
                                                in_offset=bass.IndirectOffsetOnAxis(ap=idx[:, q, a:a + 1], axis=0)
                                                ).then_inc(s_gath[q][a // HT], 16)

            sweep(pool, routed, 4, 6)

            def final(g, p):
                wait(pool, s_flast, g - 1)
                wait(pool, s_fln, g - 1)
                wait_apart(pool, s_fmv, g + 1)
                pool.tensor_scalar(fveps[:, p], fmv[:, p, :, 1], LN_EPS, None, ALU.add).then_inc(s_fveps, 1)
                wait(pool, s_fveps, g + 1)
                pool.tensor_tensor(frstd[:, p], fveps[:, p], neghalf[:, :], ALU.pow).then_inc(s_frstd, 1)

            for g in range(2):
                final(g, g)
            with pool.Fori(1, NG // 2) as j:
                final(j * 2, 0)
                final(j * 2 + 1, 1)

        @block.scalar
        def _(act):
            for row in (0, 32):
                act.dma_start(brow_s[row:row + 1, 0:2 * TPB * D], brow).then_inc(s_wbias, 16)
            act.dma_start(bcol[:, :], bcols).then_inc(s_wproj, 16)
            act.dma_start(wq_s[:, :], wq).then_inc(s_wproj, 16)
            act.wait_ge(s_wbias, 16 * 2)
            act.wait_ge(s_dve0, NDVE0)
            act.wait_ge(s_pool0, NPOOL0)
            for n in range(2):
                for row in (0, 32):
                    act.activation(bpair[row:row + 1, n, :], brow_s[row:row + 1, n * TPB * D:(n + 1) * TPB * D], ACT.Copy).then_inc(s_bhi, 1)
            act.wait_ge(s_qb, 2)

            def attention(i, par):
                b, q = i - 1, 1 - par
                if live(i):
                    wait(act, s_kps, i + 1)
                    wait(act, s_kf, i - 1)
                    act.activation(nk[:, par], psK[:, :].rearrange("p (t d) -> p t d", d=D), ACT.Relu, scale=-1.0).then_inc(s_nk, 1)
                    wait(act, s_nk, i + 1)
                    act.activation(nk[:, par], nk[:, par], ACT.Exp, scale=-1.0).then_inc(s_ek, 1)
                    wait(act, s_vps, i + 1)
                    wait(act, s_kbps, i - 1)
                    act.activation(v1[:, par, :, 0:D], psV[:, :].rearrange("p (t d) -> p t d", d=D), ACT.Copy).then_inc(s_v, 1)
                if live(i):
                    wait(act, s_qps, i + 1)
                    wait(act, s_qf, i - 1)
                    act.activation(nq[:, par], psQ[:, :], ACT.Relu, bias=nqbias[:, :], scale=-1.0).then_inc(s_nq, 1)
                    wait(act, s_nq, i + 1)
                    act.activation(nq[:, par], nq[:, par], ACT.Exp, scale=-1.0).then_inc(s_eq, 1)
                if live(i):
                    wait(act, s_gps, i + 1)
                    wait(act, s_y, i - 1)
                    act.activation(gate[:, par], psG[:, :].rearrange("p (t d) -> p t d", d=D), ACT.Tanh, scale=0.5).then_inc(s_gate, 1)
                if live(b):
                    wait(act, s_ytps, b + 1)
                    wait(act, s_ops, b - 1)
                    act.activation(yT[:, q], psYT, ACT.Copy).then_inc(s_yT, 1)
                if live(i - 2):
                    wait(act, s_x1tps, i - 1)
                    wait(act, s_lgps, i - 3)
                    wait(act, s_X1T, i - 3)
                    act.activation(x1Ts[:, par], psOT[:, :], ACT.Copy).then_inc(s_x1Ts, 1)
                if isinstance(i, int) and i == NB:
                    act.wait_ge(s_soft, 2)
                    act.activation(LG[:, 0:8 * SPLIT, :], LG[:, 0:8 * SPLIT, :], ACT.Exp).then_inc(s_exp, 1)
                    act.wait_ge(s_wlater, 16 * NLATER)
                    act.activation(iota16[:, :], SE[:, :], ACT.Copy).then_inc(s_iota, 1)
                if live(i - 2):
                    wait(act, s_lgps, i - 1)
                    act.activation(LG[:, bass.ds((i - 2) * TPB, TPB), :], kb_lg.rearrange("p (t e) -> p t e", e=E),
                                   ACT.Copy).then_inc(s_lg, 1)
                    act.activation(X1T[:, bass.ds((i - 2) * SEQ, SEQ)], x1Ts[:, par], ACT.Copy).then_inc(s_X1T, 1)

            sweep(act, attention, LAG)
            act.wait_ge(s_soft, SOFT + 2)
            act.activation(LG[:, 8 * SPLIT:NT, :], LG[:, 8 * SPLIT:NT, :], ACT.Exp).then_inc(s_exp, 1)
            def shared(i, par):
                b, q = i - 1, 1 - par
                if live(i):
                    for c in range(SC):
                        wait(act, s_sgps, i * SC + c + 1)
                        wait(act, s_hs, (i - 1) * SC + c + 1)
                        act.activation(sgg[:, c], psSG[c][:, :], ACT.Gelu).then_inc(s_sgg, 1)
                        wait(act, s_sups, i * SC + c + 1)
                        act.activation(suc[:, c], psSU[c][:, :], ACT.Copy).then_inc(s_suc, 1)
                if isinstance(i, int) and i == 0:
                    act.wait_ge(s_sT, 1)
                    act.wait_ge(s_iota, 1)
                    act.activation(SE[:, :].rearrange("p (h n) -> p h n", h=2), wide[:, :, :], ACT.Copy).then_inc(s_SE, 1)
                if live(b):
                    wait(act, s_sops, b + 1)
                    if not (isinstance(b, int) and b < 2):
                        act.wait_ge(s_accst[q], landed(b - 2, q))
                    act.activation(so[:, q], psSO[:, :].rearrange("p (t d) -> p t d", d=D), ACT.Copy).then_inc(s_so, 1)

            sweep(act, shared, 1)

            def routed(i, par):
                b, c = i - 3, i - 2

                def high(k):
                    wait(act, s_h, b * 2 * IC + k + 1)
                    wait(act, s_eops, b * 2 - 1 + k // IC)
                    act.activation(hTh[:, k % IC, k // IC * HALF:(k // IC + 1) * HALF], hraw[:, k % 2], ACT.Copy).then_inc(s_hhi, 1)

                for k in range(2 * IC):
                    if live(b):
                        wait(act, s_ggps, b * 2 * IC + k + 1)
                        wait(act, s_h, b * 2 * IC + k - 1)
                        act.activation(gg[:, k % 2], psGG[k % 2][:, :], ACT.Gelu).then_inc(s_gg, 1)
                        if k:
                            high(k - 1)
                    if live(c) and k in WEIGHTS_AT:
                        n = WEIGHTS_AT.index(k)
                        act.wait_ge(s_wt[par], landed(c, par, 2))
                        wait(act, s_eops, (c - 1) * 2)
                        if n < 2:
                            act.activation(wguh[:, par, n, :], wgu_s[:, par, n, :], ACT.Copy).then_inc(s_whi, 1)
                        else:
                            act.activation(wdh[:, par], wd_s[:, par], ACT.Copy).then_inc(s_whi, 1)
                if live(b):
                    high(2 * IC - 1)
                for h in range(2):
                    if live(b):
                        wait(act, s_eops, b * 2 + h + 1)
                        wait(act, s_backps, b * 2 - 1 + h)
                        act.activation(eoT[:, h], psX[h][:, :], ACT.Copy).then_inc(s_eoT, 1)
                    if live(c):
                        wait(act, s_trps, c * 2 + h + 1)
                        wait(act, s_uups, (c - 1) * 2 * IC + (h + 1) * IC)
                        act.activation(xgTh[:, h * HALF:(h + 1) * HALF], psXT[h][:, :], ACT.Copy).then_inc(s_xhi, 1)

            act.wait_ge(s_acc, NB)
            sweep(act, routed, 3, 6)

            def final(g, p, tiles=FT - 1):
                wait(act, s_fshift, g + 1)
                for a in range(tiles):
                    v = X1[:, bass.ds(g * FT + a, 1), :].rearrange("p o d -> p (o d)")
                    last = act.activation(v, v, ACT.Identity, bias=fshift[:, p, a:a + 1], scale=frstd[:, p, a:a + 1])
                last.then_inc(s_fln, 1)

            with act.Fori(0, NG // 2 - 1) as j:
                final(j * 2, 0)
                final(j * 2 + 1, 1)
            final(NG - 2, 0)
            final(NG - 1, 1, FT // 2)

        @block.vector
        def _(dve):
            dve.memset(bpair[:, :, :].bitcast(F32), 0.0).then_inc(s_dve0, 1)
            dve.memset(onespair[:, :].bitcast(F32), 0.0).then_inc(s_dve0, 1)
            dve.wait_ge(s_dve0, 2)
            for row in (0, 32):
                dve.memset(onespair[row:row + 1, :].bitcast(F32), 1.0).then_inc(s_dve0, 1)
            for n in range(2):
                dve.wait_ge(s_bhi, 2 * n + 2)
                low = bpair[32:33, n, :]
                dve.tensor_tensor(low, brow_s[32:33, n * TPB * D:(n + 1) * TPB * D], low.bitcast(F32), ALU.subtract).then_inc(s_blo, 1)
            dve.wait_ge(s_wproj, 16 * NPROJ)
            dve.tensor_scalar(q1bias[:, :], bcol[:, :], 1.0, None, ALU.add).then_inc(s_qb, 1)
            dve.tensor_scalar(nqbias[:, :], bcol[:, :], -1.0, None, ALU.mult).then_inc(s_qb, 1)
            dve.wait_ge(s_qb, 2)

            def less_maximum(c0, c1, n):
                some = slice(8 * c0, 8 * c1)
                dve.wait_ge(s_lg, 8 * c1 // TPB)
                dve.tensor_reduce(stat[:, 0, some], LG[:, some, :], AX.X, ALU.max).then_inc(s_soft, 1)
                dve.wait_ge(s_soft, n + 1)
                dve.tensor_tensor(LG[:, some, :], LG[:, some, :], stat[:, 0, some].unsqueeze(2).broadcast_to([P, 8 * (c1 - c0), E]),
                                  ALU.subtract).then_inc(s_soft, 1)

            def inverse_sum(c0, c1, n):
                some = slice(8 * c0, 8 * c1)
                dve.wait_ge(s_exp, n // SOFT + 1)
                dve.tensor_reduce(stat[:, 1, some], LG[:, some, :], AX.X, ALU.add).then_inc(s_soft, 1)
                dve.wait_ge(s_soft, n + 3)
                dve.reciprocal(stat[:, 2, some], stat[:, 1, some]).then_inc(s_soft, 1)

            def scores(c0, c1, n):
                dve.wait_ge(s_soft, n + 4)
                for g in range(8):
                    tiles = slice(8 * c0 + g, 8 * c1, 8)
                    last = dve.tensor_tensor(S[:, g, c0:c1], LG[:, tiles, :], stat[:, 2, tiles].unsqueeze(2).broadcast_to([P, c1 - c0, E]), ALU.mult)
                last.then_inc(s_soft, 1)

            def attention(i, par):
                b, q = i - 1, 1 - par
                if isinstance(i, int) and i == NB + 1:
                    inverse_sum(0, SPLIT, 0)
                if live(b):
                    wait(dve, s_ndps, b + 1)
                    dve.tensor_scalar(den[:, q, 0:TPB - 1], psN3[:, :, D:ND], 2e-6, None, ALU.add)
                    dve.tensor_scalar(den[:, q, TPB - 1], kb_nd[:, D:ND], 2e-6, None, ALU.add).then_inc(s_den, 1)
                    wait(dve, s_den, b + 1)
                    dve.reciprocal(rden[:, q], den[:, q]).then_inc(s_rden, 1)
                    wait(dve, s_rden, b + 1)
                    for some, num in ((slice(0, TPB - 1), psN3[:, :, 0:D]), (slice(TPB - 1, TPB), kb_nd[:, 0:D].unsqueeze(1))):
                        zb = rden[:, q, some].unsqueeze(3).broadcast_to([P, some.stop - some.start, HEADS, HD])
                        last = dve.tensor_tensor(y1[:, q, some].rearrange("p t (h c) -> p t h c", c=HD),
                                                 num.rearrange("p t (h c) -> p t h c", c=HD), zb, ALU.mult)
                    last.then_inc(s_y1, 1)
                    wait(dve, s_y1, b + 1)
                    wait(dve, s_gate, b + 1)
                    wait(dve, s_ytps, b - 1)
                    dve.scalar_tensor_tensor(y[:, q], gate[:, q], 1.0, y1[:, q], ALU.add, ALU.mult).then_inc(s_y, 1)
                if live(i - 2):
                    wait(dve, s_rstd, i - 1)
                    for a in range(TPB):
                        last = dve.tensor_scalar(x1[:, par, a, :], x1[:, par, a, :], mv[:, par, a, 0:1],
                                                 rstd[:, par, a:a + 1], ALU.subtract, ALU.mult)
                    last.then_inc(s_ln, 1)
                if isinstance(i, int) and i == NB:
                    less_maximum(0, SPLIT, 0)
                if isinstance(i, int) and i == NB + 1:
                    scores(0, SPLIT, 0)
                if live(i):
                    wait(dve, s_ek, i + 1)
                    wait(dve, s_kbps, i - 1)
                    dve.scalar_tensor_tensor(kf[:, par], psK[:, :].rearrange("p (t d) -> p t d", d=D), 1.0, nk[:, par],
                                             ALU.add, ALU.max).then_inc(s_kf, 1)
                    wait(dve, s_eq, i + 1)
                    wait(dve, s_ndps, i - 1)
                    dve.scalar_tensor_tensor(qf[:, par], psQ[:, :], q1bias[:, :], nq[:, par], ALU.add, ALU.max).then_inc(s_qf, 1)
                    if isinstance(i, int) and i == 0:
                        dve.wait_ge(s_wattn, 16 * NATTN)
                        dve.tensor_tensor(bv_s[:, :], bv_s[:, :], headmask, ALU.mult).then_inc(s_bv, 1)
                    wait(dve, s_kbps, i + 1)
                    wait(dve, s_ndps, i - 1)
                    wait(dve, s_kvks, i)
                    dve.tensor_tensor(kvh[:, :], kb_kv[:, 0:D], headmask, ALU.mult).then_inc(s_kvh, 1)
                    dve.tensor_scalar(kvks[:, par, D:ND], headsel2, kb_kv[:, D:D + 1], None, ALU.mult)
                    dve.wait_ge(s_bv, 1)
                    wait(dve, s_kvh, i + 1)
                    dve.scalar_tensor_tensor(kvks[:, par, 0:D], bv_s[:, :], kb_kv[:, D:D + 1], kvh[:, :], ALU.mult, ALU.add).then_inc(s_kvks, 1)
                if live(b):
                    wait(dve, s_ops, b + 1)
                    wait(dve, s_xb, b + 1)
                    if not (isinstance(b, int) and b < 2):
                        dve.wait_ge(s_row[q], landed(b - 2, q))
                    wait(dve, s_X1, b - 1)
                    wait(dve, s_x1tps, b - 1)
                    dve.tensor_tensor(x1[:, q], psOT[:, :].rearrange("p (t d) -> p t d", t=TPB), xb[:, q], ALU.add).then_inc(s_r, 1)
                    wait(dve, s_r, b + 1)
                    wait(dve, s_mv, b)
                    for a in range(TPB):
                        last = dve.bn_stats(bns[:, a, :], x1[:, q, a, :])
                    last.then_inc(s_bns, 1)
                    wait(dve, s_ln, b - 1)
                    wait_apart(dve, s_bns, b + 1)
                    for a in range(TPB):
                        last = dve.bn_aggr(mv[:, q, a, :], bns[:, a, :])
                    last.then_inc(s_mv, 1)

            sweep(dve, attention, LAG)

            less_maximum(SPLIT, NC, SOFT)
            dve.tensor_copy(ident16[:, :], ident).then_inc(s_cast, 1)
            dve.tensor_copy(diff16[:, :], cst[:, C_DIFF:C_DIFF + P]).then_inc(s_cast, 1)
            inverse_sum(SPLIT, NC, SOFT)
            scores(SPLIT, NC, SOFT)

            halves = SE[:, :].bitcast(U16).rearrange("p (n h) -> p n h", h=2)
            top_unit, rest_unit = float(4 ** (NTOP - 1)), float(4 ** (NREST - 1))
            dve.memset(unit[:, 0, :], top_unit).then_inc(s_bit, 1)
            dve.memset(quota[:, :], float(CAP)).then_inc(s_quota, 1)
            dve.wait_ge(s_pool0, NPOOL0)
            dve.tensor_scalar(cand[:, :], times[:, :], top_unit, None, ALU.mult).then_inc(s_cand, 1)
            dve.wait_ge(s_SE, 1)
            dve.tensor_copy(top[:, :], halves[:, :, 1]).then_inc(s_top, 1)
            dve.wait_ge(s_bit, 1)
            dve.wait_ge(s_quota, 1)
            dve.wait_ge(s_top, 1)

            def round_of(bits, n, par):
                q, again = 1 - par, int(bits is rest)
                dve.wait_ge(s_cand, n + again)
                for m in range(3):
                    last = dve.tensor_scalar((junk, gtm, eqm)[m][:, :], bits[:, :], cand[:, m + 1:m + 2], None, ALU.is_ge, ALU.add,
                                             accum_out=cnt[:, m:m + 1])
                last.then_inc(s_cnt, 1)
                dve.tensor_scalar(unit[:, q, :], unit[:, par, :], 0.25, None, ALU.mult).then_inc(s_bit, 1)
                dve.wait_ge(s_bit, n + 1 + again)
                dve.scalar_tensor_tensor(cand_next[:, :], times[:, :], unit[:, q, 0:1], cand[:, 0:1].broadcast_to([P, 4]),
                                         ALU.mult, ALU.add).then_inc(s_next, 1)
                dve.wait_ge(s_tot, n + again)
                dve.tensor_scalar(ge[:, :], psTOT[:, 0:3], quota[:, :], None, ALU.is_ge, ALU.add, accum_out=step[:, :]).then_inc(s_step, 1)
                dve.wait_ge(s_next, n)
                dve.wait_ge(s_step, n)
                dve.scalar_tensor_tensor(cand[:, :], unit[:, par, :], step[:, :], cand_next[:, :], ALU.mult, ALU.add).then_inc(s_cand, 1)

            round_of(top, 1, 0)
            round_of(top, 2, 1)
            with dve.Fori(1, NTOP // 2) as j:
                round_of(top, j * 2 + 1, 0)
                round_of(top, j * 2 + 2, 1)
            round_of(top, NTOP, 0)
            dve.wait_ge(s_cand, NTOP + 1)
            dve.tensor_copy(thrf[:, :], cand[:, 0:1]).then_inc(s_thr, 1)
            dve.wait_ge(s_thr, 1)
            dve.tensor_scalar(junk[:, :], top[:, :], thrf[:, :], None, ALU.is_gt, ALU.add, accum_out=cnt[:, 0:1]).then_inc(s_cnt, 1)
            dve.scalar_tensor_tensor(rest[:, :], top[:, :], thrf[:, :], halves[:, :, 0], ALU.is_equal, ALU.mult).then_inc(s_top, 1)
            dve.tensor_scalar(thr_top[:, :], thrf[:, :], float(2 ** 16), None, ALU.mult).then_inc(s_thr, 1)
            dve.memset(unit[:, 1, :], rest_unit).then_inc(s_bit, 1)
            dve.tensor_scalar(cand[:, :], times[:, :], rest_unit, None, ALU.mult).then_inc(s_cand, 1)
            dve.wait_ge(s_tot, NTOP + 1)
            dve.tensor_scalar(quota[:, :], psTOT[:, 0:1], -1.0, float(CAP), ALU.mult, ALU.add).then_inc(s_quota, 1)
            dve.wait_ge(s_quota, 2)
            dve.wait_ge(s_top, 2)
            dve.wait_ge(s_bit, NTOP + 2)
            with dve.Fori((NTOP + 1) // 2, (NTOP + 1 + NREST) // 2) as j:
                round_of(rest, j * 2, 1)
                round_of(rest, j * 2 + 1, 0)
            dve.wait_ge(s_cand, NTOP + NREST + 2)
            dve.tensor_copy(thr_rest[:, :], cand[:, 0:1]).then_inc(s_thr, 1)
            dve.wait_ge(s_thr, 3)
            dve.tensor_tensor(thr[:, :], thr_top[:, :], thr_rest[:, :], ALU.bitwise_or).then_inc(s_thr, 1)
            dve.wait_ge(s_thr, 4)
            vth = thr[:, :].bitcast(F32)

            dve.tensor_scalar(gtm[:, :], SE[:, :], vth, None, ALU.is_gt, ALU.add, accum_out=tiecnt[:, 0:1]).then_inc(s_pick, 1)
            dve.tensor_scalar(eqm[:, :], SE[:, :], vth, None, ALU.is_equal, ALU.add, accum_out=tiecnt[:, 1:2]).then_inc(s_pick, 1)
            dve.wait_ge(s_pickps, 1)
            dve.tensor_scalar(need[:, :], psTOT[:, 0:1], -1.0, float(CAP), ALU.mult, ALU.add).then_inc(s_pick, 1)
            dve.tensor_copy(tieoff[:, :], psTOT[:, 1:2]).then_inc(s_pick, 1)
            dve.wait_ge(s_pick, 4)
            dve.tensor_tensor_scan(rank[:, :], eqm[:, :], eqm[:, :], tieoff[:, :], ALU.add, ALU.max).then_inc(s_pick, 1)
            dve.wait_ge(s_pick, 5)
            dve.scalar_tensor_tensor(tiesel[:, :], rank[:, :], need[:, :], eqm[:, :], ALU.is_le, ALU.mult).then_inc(s_pick, 1)
            dve.wait_ge(s_pick, 6)
            dve.tensor_tensor(sel[:, :], tiesel[:, :], gtm[:, :], ALU.add).then_inc(s_pick, 1)
            dve.wait_ge(s_pickps, 2)
            selT = psTOT[:, :].bitcast(F16).rearrange("p (g c e) -> p g c e", g=8, c=8)
            for c in range(8):
                last = dve.tensor_copy(M[:, :, c * 8:c * 8 + 8], selT[:, :, c, :].rearrange("p g e -> p e g"))
            last.then_inc(s_pick, 1)
            dve.wait_ge(s_pick, 8)
            flat = [t[:, :, :].rearrange("p e t -> p (e t)") for t in (M, G)]
            dve.tensor_tensor_scan(flat[1], flat[0], flat[0], 0.0, ALU.add, ALU.max).then_inc(s_pick, 1)
            dve.wait_ge(s_pick, 9)
            dve.tensor_copy(gprev[:, 1:E], G[:, 0:E - 1, NT - 1]).then_inc(s_pick, 1)
            dve.wait_ge(s_pick, 10)
            dve.tensor_tensor(nsel[:, :], G[:, :, NT - 1], gprev[:, :], ALU.subtract).then_inc(s_pick, 1)
            dve.wait_ge(s_pickps, 3)
            dve.tensor_copy(off[:, 0:E], psTOT[:, 0:E]).then_inc(s_pick, 1)
            dve.wait_ge(s_pick, 12)
            dve.tensor_tensor(base[:, :], off[:, 0:E], gprev[:, :], ALU.subtract).then_inc(s_pick, 1)
            dve.wait_ge(s_pick, 13)
            dve.tensor_tensor(C16[:, :, :], G[:, :, :], base[:, :].unsqueeze(2).broadcast_to([P, E, NT]), ALU.add).then_inc(s_pick, 1)
            dve.tensor_copy(tab[:, :, NT], cst[:, C_BLK:C_BLK + E]).then_inc(s_pick, 1)

            def first_slots(e):
                wait_apart(dve, s_cps, e)
                dve.tensor_scalar(U[:, :], iota16[:, :], off[:, bass.ds(e, 1)], None, ALU.is_ge).then_inc(s_U, 1)

            dve.wait_ge(s_iota, 1)
            first_slots(0)
            dve.wait_ge(s_pickps, 4)
            for h in range(2):
                last = dve.tensor_copy(tab[:, h * 8:h * 8 + 8, 0:NT], wide[:, h, :].rearrange("p (e t) -> p e t", t=NT))
            last.then_inc(s_pick, 1)

            def routed(i, par):
                b, c, q = i - 3, i - 2, 1 - par

                def weights_low(n):
                    wait(dve, s_whi, c * 3 + n + 1)
                    if n < 2:
                        dve.tensor_tensor(wgul[:, par, n, :], wgu_s[:, par, n, :], wguh[:, par, n, :].bitcast(F32),
                                          ALU.subtract).then_inc(s_wlo, 1)
                    else:
                        dve.tensor_tensor(wdl[:, par], wd_s[:, par], wdh[:, par].bitcast(F32), ALU.subtract).then_inc(s_wlo, 1)

                def low(k):
                    part = slice(k // IC * HALF, (k // IC + 1) * HALF)
                    wait(dve, s_hhi, b * 2 * IC + k + 1)
                    dve.tensor_tensor(hTl[:, k % IC, part], hraw[:, k % 2], hTh[:, k % IC, part].bitcast(F32),
                                      ALU.subtract).then_inc(s_hlo, 1)

                if live(i):
                    first_slots(i + 1)
                for k in range(2 * IC):
                    if live(b):
                        wait(dve, s_gg, b * 2 * IC + k + 1)
                        wait(dve, s_uups, b * 2 * IC + k + 1)
                        wait(dve, s_hlo, b * 2 * IC + k - 1)
                        dve.tensor_tensor(hraw[:, k % 2], gg[:, k % 2], psUU[k % 2][:, :], ALU.mult).then_inc(s_h, 1)
                        if k:
                            low(k - 1)
                    if live(c) and k == 0:
                        weights_low(0)
                if live(b):
                    low(2 * IC - 1)
                if live(c):
                    if not (isinstance(c, int) and c < 2):
                        dve.wait_ge(s_scat[par], landed(c - 2, par, ST))
                    wait_apart(dve, s_idx, c + 1)
                    dve.tensor_copy(idxs[:, par], idx[:, par]).then_inc(s_idxs, 1)
                if live(i):
                    cs = wide[:, :, 0:HT * (NT + 1)].rearrange("p h (a t) -> p h a t", t=NT + 1)
                    wait(dve, s_cps, i + 1)
                    wait(dve, s_cntt, i)
                    for h in range(2):
                        last = dve.tensor_tensor(cmp[:, h * HT:h * HT + HT, :], cs[:, h, :, 0:NT],
                                                 slotno[:, h * HT:h * HT + HT].unsqueeze(2).broadcast_to([P, HT, NT]), ALU.is_le)
                    last.then_inc(s_cmp, 1)
                    wait(dve, s_cmp, i + 1)
                    wait(dve, s_idx, i)
                    dve.tensor_reduce(cntt[:, :], cmp[:, :, :], AX.X, ALU.add).then_inc(s_cntt, 1)
                    if live(c):
                        wait(dve, s_idxs, c + 1)
                        for h in range(2):
                            dve.wait_ge(s_gath[par][h], landed(c, par, HT))
                    wait(dve, s_cntt, i + 1)
                    dve.scalar_tensor_tensor(idx[:, par].rearrange("p (h a) -> p h a", h=2),
                                             cntt[:, :].rearrange("p (h a) -> p h a", h=2), float(P), cs[:, :, :, NT],
                                             ALU.mult, ALU.add).then_inc(s_idx, 1)
                if live(c):
                    for h in range(2):
                        part = slice(h * HALF, (h + 1) * HALF)
                        wait(dve, s_xhi, c * 2 + h + 1)
                        dve.tensor_tensor(xgTl[:, part], psXT[h][:, :], xgTh[:, part].bitcast(F32), ALU.subtract).then_inc(s_xlo, 1)
                        if h == 0:
                            weights_low(1)
                            weights_low(2)
                if live(b):
                    for h in range(2):
                        wait(dve, s_backps, b * 2 + h + 1)
                        if h == 0 and not (isinstance(b, int) and b < 2):
                            dve.wait_ge(s_scat[q], landed(b - 2, q, ST))
                        w = score[:, q, h * HT:h * HT + HT].unsqueeze(2).broadcast_to([P, HT, D])
                        dve.tensor_tensor(eo[:, q, h * HT:h * HT + HT, :], psX[h][:, :].rearrange("p (a d) -> p a d", d=D), w,
                                          ALU.mult).then_inc(s_eo, 1)
                if live(c):
                    wait(dve, s_eo, (c - 1) * 2)
                    for h in range(2):
                        dve.wait_ge(s_gath[par][h], landed(c, par, HT))
                    wait_apart(dve, s_trps, c * 2 + 2)
                    dve.tensor_copy(score[:, par].unsqueeze(2), xg[:, par, :, bass.ds(c + D, 1)]).then_inc(s_score, 1)

            def shared_product(i, par):
                dve.wait_ge(s_hs, i * SC)
                for c in range(SC):
                    dve.wait_ge(s_suc, i * SC + c + 1)
                    dve.wait_ge(s_sops, i - 1)
                    dve.tensor_tensor(hs[:, par, c], sgg[:, c], suc[:, c], ALU.mult).then_inc(s_hs, 1)

            def shared_sum(b, q):
                dve.wait_ge(s_so, b + 1)
                dve.wait_ge(s_acc, b)
                dve.tensor_tensor(so[:, q], so[:, q], X1[:, b * TPB:(b + 1) * TPB, :], ALU.add).then_inc(s_acc, 1)

            routed(0, 0)
            shared_product(NB - 1, 1)
            shared_sum(NB - 2, 0)
            routed(1, 1)
            shared_sum(NB - 1, 1)
            sweep(dve, routed, 3, 6, first=2)

            def final(g, k):
                p = k % 2
                dve.wait_ge(s_fin[k], 16 * (g // FG + 1) if isinstance(g, int) else (g - k) * 4 + 16)
                wait(dve, s_fmv, g)
                for a in range(FT):
                    last = dve.bn_stats(fbns[:, a, :], X1[:, bass.ds(g * FT + a, 1), :].rearrange("p o d -> p (o d)"))
                last.then_inc(s_fbns, 1)
                wait(dve, s_flast, g - 1)
                wait_apart(dve, s_fbns, g + 1)
                for a in range(FT):
                    last = dve.bn_aggr(fmv[:, p, a, :], fbns[:, a, :])
                last.then_inc(s_fmv, 1)

            def shift(g, k, tiles=FT - 1):
                p = k % 2
                wait(dve, s_frstd, g + 1)
                wait(dve, s_fln, g - 1)
                dve.scalar_tensor_tensor(fshift[:, p], fmv[:, p, :, 0], -1.0, frstd[:, p], ALU.mult, ALU.mult).then_inc(s_fshift, 1)
                for a in range(tiles, FT):
                    v = X1[:, bass.ds(g * FT + a, 1), :].rearrange("p o d -> p (o d)")
                    last = dve.tensor_scalar(v, v, fmv[:, p, a, 0:1], frstd[:, p, a:a + 1], ALU.subtract, ALU.mult)
                last.then_inc(s_flast, 1)

            for k in range(FG):
                final(k, k)
                if k:
                    shift(k - 1, k - 1)
            with dve.Fori(1, NG // FG) as j:
                for k in range(FG):
                    final(j * FG + k, k)
                    shift(j * FG + k - 1, (k - 1) % FG)
            shift(NG - 1, FG - 1, FT // 2)

        @block.tensor
        def _(pe):
            pe.wait_ge(s_wproj, 16 * NPROJ)
            pe.wait_ge(s_dve0, NDVE0)
            pe.wait_ge(s_pool0, NPOOL0)

            def project(ps, i, par, n, bias=None):
                if bias is not None:
                    if isinstance(i, int) and i == 0:
                        pe.wait_ge(s_blo, bias + 1)
                    pe.matmul(ps[:, :], onespair[:, :], bpair[:, bias, :], start=True, stop=False)
                for a in range(TPB):
                    last = pe.matmul(ps[:, a * D:(a + 1) * D], xTb[:, par, a * P:(a + 1) * P], wkvg_s[:, n * D:(n + 1) * D],
                                     start=(bias is None), stop=(bias is None or a == TPB - 1))
                return last

            def attention(i, par):
                b, q = i - 1, 1 - par
                if live(i):
                    pe.wait_ge(s_xT[par], landed(i, par))
                    wait(pe, s_kf, i)
                    project(psK, i, par, 0, 0).then_inc(s_kps, 1)
                    wait(pe, s_v, i)
                    project(psV, i, par, 1).then_inc(s_vps, 1)
                    wait(pe, s_qf, i)
                    pe.matmul(psQ[:, :], wq_s[:, :], xTb[:, par], start=True, stop=True).then_inc(s_qps, 1)
                    wait(pe, s_gate, i)
                    project(psG, i, par, 2, 1).then_inc(s_gps, 1)
                if isinstance(i, int) and i == 1:
                    pe.wait_ge(s_wattn, 16 * NATTN)
                if live(b):
                    wait(pe, s_y, b + 1)
                    wait(pe, s_yT, b)
                    for a in range(TPB):
                        last = pe.transpose(psYT[:, a * P:(a + 1) * P], y[:, q, a, :], ident)
                    last.then_inc(s_ytps, 1)
                if live(i - 2):
                    wait(pe, s_ln, i - 1)
                    wait(pe, s_r, i - 1)
                    for a in range(TPB):
                        last = pe.transpose(psOT[:, a * P:(a + 1) * P], x1[:, par, a, :], ident)
                    last.then_inc(s_x1tps, 1)
                if live(i):
                    wait(pe, s_kf, i + 1)
                    wait(pe, s_v, i + 1)
                    wait(pe, s_y1, i)
                    wait(pe, s_lg, i - 2)
                    for a in range(TPB):
                        last = pe.matmul(kb_kv, kf[:, par, a, :], v1[:, par, a, :], start=(a == 0), stop=(a == TPB - 1))
                    last.then_inc(s_kbps, 1)
                if live(b):
                    wait(pe, s_yT, b + 1)
                    wait(pe, s_x1Ts, b)
                    for a in range(TPB):
                        last = pe.matmul(psOT[:, a * D:(a + 1) * D], yT[:, q, a * P:(a + 1) * P], wo_s[:, :], start=True, stop=True)
                    last.then_inc(s_ops, 1)
                if live(i - 2):
                    wait(pe, s_x1Ts, i - 1)
                    wait(pe, s_kvks, min(i + 1, NB) if isinstance(i, int) else i + 1)
                    for a in range(TPB):
                        last = pe.matmul(kb_lg[:, a * E:(a + 1) * E], x1Ts[:, par, a * P:(a + 1) * P], gateT_s[:, :], start=True, stop=True)
                    last.then_inc(s_lgps, 1)
                if live(i):
                    wait(pe, s_kvks, i + 1)
                    wait(pe, s_qf, i + 1)
                    for a in range(TPB):
                        nd = psN3[:, a, :] if a < TPB - 1 else kb_nd
                        if a == TPB - 1:
                            wait(pe, s_lg, i - 1)
                        last = pe.matmul(nd, qf[:, par, a * P:(a + 1) * P], kvks[:, par], start=True, stop=True)
                    last.then_inc(s_ndps, 1)

            def count(n):
                wait(pe, s_cnt, n)
                pe.matmul(psTOT[:, 0:3], same_expert, cnt[:, :], start=True, stop=True).then_inc(s_tot, 1)


            def shared(i, par, counts=None, middle=None):
                b, q = i - 1, 1 - par

                def between(n):
                    if counts and counts[n] is not None:
                        count(counts[n])

                if live(i):
                    for c in range(SC):
                        wait(pe, s_sgg, i * SC + c - 1)
                        pe.matmul(psSG[c][:, :], wsgu_s[:, 0, c * P:(c + 1) * P], X1T[:, bass.ds(i * SEQ, SEQ)],
                                  start=True, stop=True).then_inc(s_sgps, 1)
                        wait(pe, s_suc, i * SC + c - 1)
                        pe.matmul(psSU[c][:, :], wsgu_s[:, 1, c * P:(c + 1) * P], X1T[:, bass.ds(i * SEQ, SEQ)],
                                  start=True, stop=True).then_inc(s_sups, 1)
                        between(c)
                if middle:
                    middle()
                if live(b):
                    wait(pe, s_hs, b * SC + SC)
                    wait(pe, s_so, b)
                    for a in range(TPB):
                        for c in range(SC):
                            last = pe.matmul(psSO[:, a * D:(a + 1) * D], hs[:, q, c, a * P:(a + 1) * P], wsd_s[:, c, :],
                                             start=(c == 0), stop=(c == SC - 1))
                    last.then_inc(s_sops, 1)
                    between(2)

            def turn_scores():
                pe.wait_ge(s_soft, 2 * SOFT)
                for g in range(8):
                    last = pe.transpose(wide[:, g // 4, g % 4 * P:(g % 4 + 1) * P], S[:, g].rearrange("p c e -> p (c e)"), ident)
                last.then_inc(s_sT, 1)

            def tie_sums():
                pe.wait_ge(s_pick, 2)
                pe.matmul(psTOT[:, 0:1], same_expert, tiecnt[:, 0:1], start=True, stop=True)
                pe.matmul(psTOT[:, 1:2], earlier_run, tiecnt[:, 1:2], start=True, stop=True).then_inc(s_pickps, 1)

            def turn_selection():
                pe.wait_ge(s_pick, 7)
                pe.wait_ge(s_cast, 2)
                for g in range(8):
                    last = pe.transpose(psTOT[:, :].bitcast(F16)[:, g * P:(g + 1) * P], sel[:, g * P:(g + 1) * P], ident16[:, :])
                last.then_inc(s_pickps, 1)

            def earlier_partitions():
                pe.wait_ge(s_pick, 11)
                pe.matmul(psTOT[:, 0:E], upper, nsel[:, :], start=True, stop=True).then_inc(s_pickps, 1)

            def differences():
                pe.wait_ge(s_pick, 15)
                pe.wait_ge(s_SE, 1)
                for h in range(2):
                    last = pe.matmul(wide[:, h, :], diff16[:, :], C16[:, h * 8:h * 8 + 8, :].rearrange("p e t -> p (e t)"), start=True, stop=True)
                last.then_inc(s_pickps, 1)

            def slots(i):
                if isinstance(i, int) and i == 0:
                    pe.wait_ge(s_pick, 16)
                wait(pe, s_U, i + 1)
                wait(pe, s_idx, i)
                for a in range(ST):
                    last = pe.matmul(wide[:, a // HT, a % HT * (NT + 1):(a % HT + 1) * (NT + 1)], U[:, a * P:(a + 1) * P],
                                     tab[:, bass.ds(i, 1), :].rearrange("p o t -> p (o t)"), start=True, stop=True)
                last.then_inc(s_cps, 1)

            sweep(pe, attention, 0)
            for s in (s_kf, s_v, s_gate, s_qf):
                pe.wait_ge(s, NB)
            pe.wait_ge(s_wlater, 16 * NLATER)
            shared(0, 0)
            attention(NB, 0)
            attention(NB + 1, 1)
            for s in (s_yT, s_y1, s_r, s_x1Ts, s_X1T, s_lg):
                pe.wait_ge(s, NB)
            turn_scores()
            shared(1, 1, (1, None, 2))
            with pe.Fori(1, 5) as j:
                shared(j * 2, 0, (None, j * 3, None))
                shared(j * 2 + 1, 1, (j * 3 + 1, None, j * 3 + 2))
            shared(10, 0, (None, NCOUNT - 1, None))
            shared(11, 1, (NCOUNT, None, None))
            tie_sums()
            shared(12, 0)
            turn_selection()
            shared(13, 1, middle=earlier_partitions)
            differences()
            shared(14, 0, middle=lambda: slots(0))
            shared(15, 1, middle=lambda: slots(1))
            shared(16, 0)
            for s, n in ((s_sgg, SC), (s_suc, SC), (s_so, 1)):
                pe.wait_ge(s, NB * n)
            pe.wait_ge(s_pick, 16)

            def product(ps, lhs, rhs, first, last):
                pe.matmul(ps, lhs[0], rhs[0], start=first, stop=False)
                pe.matmul(ps, lhs[0], rhs[1], start=False, stop=False)
                return pe.matmul(ps, lhs[1], rhs[0], start=False, stop=last)

            def turn_back(b, h):
                wait(pe, s_eoT, b * 2 + h + 1)
                for a in range(HT):
                    last = pe.transpose(psX[h][:, a * P:(a + 1) * P], eoT[:, h, a * P:(a + 1) * P], ident)
                last.then_inc(s_backps, 1)

            def routed(i, par):
                b, c, q = i - 3, i - 2, 1 - par
                if live(i) and not (isinstance(i, int) and i < 2):
                    slots(i)
                if live(b):
                    wait(pe, s_wlo, b * 3 + 3)
                    for h in range(2):
                        part = slice(h * HALF, (h + 1) * HALF)
                        if h == 0:
                            wait(pe, s_xlo, b * 2 + 1)
                        for m in range(IC):
                            k = h * IC + m
                            if k == 1:
                                wait(pe, s_xlo, b * 2 + 2)
                            chunk = slice(m * P, (m + 1) * P)
                            wait(pe, s_gg, b * 2 * IC + k - 1)
                            wait(pe, s_h, b * 2 * IC + k - 1)
                            x2 = (xgTh[:, part], xgTl[:, part])
                            product(psGG[k % 2][:, :], (wguh[:, q, 0, chunk], wgul[:, q, 0, chunk]), x2, True, True).then_inc(s_ggps, 1)
                            product(psUU[k % 2][:, :], (wguh[:, q, 1, chunk], wgul[:, q, 1, chunk]), x2, True, True).then_inc(s_uups, 1)
                for h in range(2):
                    if live(b):
                        wait(pe, s_hlo, b * 2 * IC + (h + 1) * IC)
                        wait(pe, s_eo, b * 2 - 1 + h)
                        part = slice(h * HALF, (h + 1) * HALF)
                        for m in range(IC):
                            last = product(psX[h][:, :], (wdh[:, q, m, :], wdl[:, q, m, :]), (hTh[:, m, part], hTl[:, m, part]),
                                           m == 0, m == IC - 1)
                        last.then_inc(s_eops, 1)
                    if live(c):
                        pe.wait_ge(s_gath[par][h], landed(c, par, HT))
                        wait(pe, s_gg, (c - 1) * 2 * IC + 2 * IC - 1 + h)
                        for a in range(HT):
                            last = pe.transpose(psXT[h][:, a * P:(a + 1) * P], xg[:, par, h * HT + a, 0:D], ident)
                        last.then_inc(s_trps, 1)
                    elif live(b):
                        turn_back(b, h)
                if live(b) and live(c):
                    for h in range(2):
                        turn_back(b, h)

            sweep(pe, routed, 3, 6)


def kernel(**inputs):
    import concourse.bacc as bacc
    from concourse.bass_utils import run_bass_kernel_spmd

    g = {k: np.ascontiguousarray(v) for k, v in inputs.items()}
    arrays = {
        "x": g["L0_attn_x"],
        "xT": g["L0_attn_x"].transpose(0, 2, 1),
        "wq": g["L0_attn_wq_w"],
        "wkvg": np.concatenate([g["L0_attn_wk_w"], g["L0_attn_wv_w"], g["L0_attn_wg_w"]], axis=1),
        "wo": g["L0_attn_out_w"],
        "bcols": g["L0_attn_wq_b"][:, None],
        "brow": np.tile(np.stack([g["L0_attn_wk_b"], g["L0_attn_wg_b"]]), (1, TPB)).reshape(1, -1),
        "bv": np.broadcast_to(g["L0_attn_wv_b"][None, :], (P, D)),
        "bo": np.broadcast_to(g["L0_attn_out_b"][None, :], (P, D)),
        "consts": constants(),
        "iota": np.broadcast_to(np.arange(CAP, dtype=np.float32)[None, :], (P, CAP)),
        "gateT": g["L0_ffn_gate_w"].T,
        "wsgu": np.stack([g["L0_ffn_Sg"].T, g["L0_ffn_Su"].T], axis=1),
        "wsd": g["L0_ffn_Sd"].T.reshape(SC, P, D).transpose(1, 0, 2),
        "wgu": np.stack([g["L0_ffn_Wg"].transpose(0, 2, 1), g["L0_ffn_Wu"].transpose(0, 2, 1)], axis=2),
        "wd": g["L0_ffn_Wd"].transpose(0, 2, 1).reshape(E, IC, P, D).transpose(0, 2, 1, 3),
    }
    arrays = {f"in_{n}": np.ascontiguousarray(a) for n, a in arrays.items()}
    nc = bacc.Bacc("TRN2", target_bir_lowering=False, num_devices=1)
    args = [nc.dram_tensor(n, a.shape, mybir.dt.from_np(a.dtype), kind="ExternalInput").ap() for n, a in arrays.items()]
    args.append(nc.dram_tensor("out", (NB, SEQ, D), F32, kind="ExternalOutput").ap())
    program(nc, *args)
    r = run_bass_kernel_spmd(nc, [arrays], core_ids=[0])
    return r.results[0]["out"]
```
